# Optimizing a Trainium2 kernel written in Bass

```python
import numpy as np
import jax
import jax.numpy as jnp

def _softmax(x, axis=-1):
    return jax.nn.softmax(x, axis=axis)

def _gelu(x):
    return jax.nn.gelu(x, approximate=True)

def _silu(x):
    return jax.nn.silu(x)

def _sigmoid(x):
    return jax.nn.sigmoid(x)

def _layernorm(x, axis=-1, eps=1e-05):
    m = jnp.mean(x, axis=axis, keepdims=True)
    v = jnp.var(x, axis=axis, keepdims=True)
    return (x - m) / jnp.sqrt(v + eps)

def _scatter_add(tgt, idx, src, axis=0):
    return tgt.at[idx].add(src)

def _segment_sum(src, seg, n):
    return jax.ops.segment_sum(src, seg, n)
kernel_name = 'mk_xattn_ffn_d4_seqx_r4_dc8f76'

def setup_inputs(seed: int=0):
    np.random.seed(seed)
    _w = jnp.asarray

    def _rec_inputs():
        import jax
        import jax.numpy as jnp
        _rk = jax.random.key(seed)
        x = -0.0003929 + 0.9999 * jax.random.normal(jax.random.fold_in(_rk, 1), (16, 112, 256), jnp.float32)
        _lenS = 112 - jax.random.randint(jax.random.fold_in(_rk, 7), (16,), 0, max(1, 112 // 4) + 1, jnp.int32)
        _lenS2 = 375 - jax.random.randint(jax.random.fold_in(_rk, 8), (16,), 0, max(1, 375 // 4) + 1, jnp.int32)
        _ctx_1024P = jax.random.normal(jax.random.fold_in(_rk, 11), (16, 16, 256), jnp.float32)
        _ctx_1024c = jax.random.dirichlet(jax.random.fold_in(_rk, 511), 0.3 * jnp.ones((16,), jnp.float32), (16, 375))
        _ctx_1024t = jnp.einsum('bsk,bkd->bsd', _ctx_1024c, _ctx_1024P)
        _ctx_1024t = _ctx_1024t * jax.lax.rsqrt(jnp.mean(jnp.square(_ctx_1024t)) + 1e-12) * 0.953939
        ctx_1024 = 2.81802e-05 + 1.00001 * (_ctx_1024t + 0.3 * jax.random.normal(jax.random.fold_in(_rk, 611), (16, 375, 256), jnp.float32))
        _validS = jnp.arange(112)[None, :] < _lenS[:, None]
        _validS2 = jnp.arange(375)[None, :] < _lenS2[:, None]
        _causal = jnp.tril(jnp.ones((112, 112), dtype=bool))
        mask_Bx1xS2_bk0 = jnp.logical_not(jnp.broadcast_to(_validS2[:, None, :], (16, 1, 375)))
        mask_BxSxS2_if1 = jnp.where(jnp.ones((16, 112, 375), dtype=bool), 1, 0).astype(jnp.int32)
        return (x, ctx_1024, mask_Bx1xS2_bk0, mask_BxSxS2_if1)
    x, ctx_1024, mask_Bx1xS2_bk0, mask_BxSxS2_if1 = _rec_inputs()

    def _L0_xattn_setup():
        import jax, jax.numpy as jnp
        import numpy as np
        B, N, D = (4, 1024, 256)
        H = 16
        HD = D // H
        EPS = 1e-06
        BASE_SPARSITY = 0.3
        KEEP = max(int((1.0 - BASE_SPARSITY) * HD), 1)
        LEAKY_SLOPE = 0.01

        def _focus(x, focusing_factor):
            x = jnp.abs(jnp.where(x >= 0, x, LEAKY_SLOPE * x)) + EPS
            nrm = x.mean(axis=-1, keepdims=True)
            return jax.nn.softmax(jnp.log(x) * focusing_factor, axis=-1) * nrm

        def _to_heads(x):
            b, n, d = x.shape
            return x.reshape(b, n, H, HD).transpose(0, 2, 1, 3).reshape(b * H, n, HD)

        def _topk_sparsify(x):
            c = x.shape[-1]
            flat = x.reshape(-1, c)
            _, idx = jax.lax.top_k(jnp.abs(flat), KEEP)
            rows = jnp.arange(flat.shape[0])[:, None]
            mask = jnp.zeros(flat.shape, dtype=bool).at[rows, idx].set(True)
            return (flat * mask).reshape(x.shape)
        key = jax.random.key(seed)
        ks = jax.random.split(key, 8)
        mk = lambda k_, shp, s: jax.random.normal(k_, shp, dtype=jnp.float32) * s
        return {'q': mk(ks[0], (B, N, D), 1.0), 'k': mk(ks[1], (B, N, D), 1.0), 'v': mk(ks[2], (B, N, D), 1.0), 'Wq': mk(ks[3], (D, D), 0.02), 'Wk': mk(ks[4], (D, D), 0.02), 'Wv': mk(ks[5], (D, D), 0.02), 'Wp': mk(ks[6], (D, D), 0.02), 'focusing_factor': jnp.asarray(3.0, dtype=jnp.float32)}
    _L0_xattn_all = _L0_xattn_setup()
    _L0_xattn_in = {k: v for k, v in _L0_xattn_all.items() if k in ('Wq', 'Wk', 'Wv', 'Wp', 'focusing_factor')}
    del _L0_xattn_all

    def _L0_ffn_setup():
        import math
        import jax, jax.numpy as jnp
        import numpy as np
        D_MODEL = 256
        D_FF = 1024
        E = 8
        K = 2
        CAP_FACTOR = 1.25
        CLAMP = 10000.0
        LN_EPS = 1e-05
        B, S = (2, 512)
        key = jax.random.key(seed)
        ks = jax.random.split(key, 6)
        b12 = math.sqrt(6.0 / (D_MODEL + 2 * D_FF))
        b3 = math.sqrt(6.0 / (D_FF + D_MODEL))
        br = 0.02 * math.sqrt(3.0)
        return {'x': jax.random.normal(ks[0], (B, S, D_MODEL), dtype=jnp.float32), 'ln_gamma': jnp.ones((D_MODEL,), jnp.float32), 'ln_beta': jnp.zeros((D_MODEL,), jnp.float32), 'router_w': jax.random.uniform(ks[1], (E, D_MODEL), jnp.float32, -br, br), 'w12': jax.random.uniform(ks[2], (E, 2 * D_FF, D_MODEL), jnp.float32, -b12, b12), 'w3': jax.random.uniform(ks[3], (E, D_MODEL, D_FF), jnp.float32, -b3, b3)}
    _L0_ffn_all = _L0_ffn_setup()
    _L0_ffn_in = {k: v for k, v in _L0_ffn_all.items() if k in ('ln_gamma', 'ln_beta', 'router_w', 'w12', 'w3')}
    del _L0_ffn_all

    def _L1_xattn_setup():
        import jax, jax.numpy as jnp
        import numpy as np
        B, S, E, H = (4, 512, 256, 16)
        DH = E // H

        def _make_heads(v, n_heads):
            b, n, e = v.shape
            return jnp.moveaxis(v.reshape(b, n, n_heads, e // n_heads), -2, 0)
        key = jax.random.key(seed)
        k1, k2, k3, k4, k5 = jax.random.split(key, 5)
        return {'query': jax.random.normal(k1, (B, S, E), dtype=jnp.float32), 'key': jax.random.normal(k2, (B, S, E), dtype=jnp.float32), 'value': jax.random.normal(k3, (B, S, E), dtype=jnp.float32), 'mask': jax.random.randint(k4, (B, 1, S), 0, 2).astype(bool), 'W_out': jax.random.normal(k5, (E, E), dtype=jnp.float32) / np.sqrt(E), 'scale': jnp.asarray(1.0, dtype=jnp.float32), 'log_C': jnp.asarray(np.log(10.0), dtype=jnp.float32)}
    _L1_xattn_all = _L1_xattn_setup()
    _L1_xattn_in = {k: v for k, v in _L1_xattn_all.items() if k in ('W_out', 'scale', 'log_C')}
    del _L1_xattn_all

    def _L1_ffn_setup():
        import jax, jax.numpy as jnp
        import numpy as np
        D_MODEL, D_FF, NUM_EXPERTS, RANK, TOP_K = (256, 1024, 8, 16, 2)
        B, S = (8, 512)

        def _expert_ffn(h, wi_w, wo_w, A, Bm):
            inter = jnp.einsum('bsd,fd->bsf', h, wi_w)
            lora = jnp.einsum('bsr,fr->bsf', jnp.einsum('bsd,rd->bsr', h, A), Bm)
            inter = jax.nn.relu(inter + lora)
            return jnp.einsum('bsf,df->bsd', inter, wo_w)
        key = jax.random.key(seed)
        ks = jax.random.split(key, 8)
        hidden_states = jax.random.normal(ks[0], (B, S, D_MODEL), dtype=jnp.float32)
        wi_w = jax.random.normal(ks[1], (D_FF, D_MODEL), dtype=jnp.float32) * (1.0 / np.sqrt(D_MODEL))
        wo_w = jax.random.normal(ks[2], (D_MODEL, D_FF), dtype=jnp.float32) * (1.0 / np.sqrt(D_FF))
        lora_As = jax.random.uniform(ks[3], (NUM_EXPERTS, RANK, D_MODEL), dtype=jnp.float32, minval=-1.0, maxval=1.0) / np.sqrt(D_MODEL)
        lora_Bs = jax.random.normal(ks[4], (NUM_EXPERTS, D_FF, RANK), dtype=jnp.float32) * 0.02
        top_k_indices = jnp.arange(TOP_K, dtype=jnp.int32)
        top_k_values = jax.random.uniform(ks[5], (TOP_K,), dtype=jnp.float32)
        return {'hidden_states': hidden_states, 'wi_w': wi_w, 'wo_w': wo_w, 'lora_As': lora_As, 'lora_Bs': lora_Bs, 'top_k_indices': top_k_indices, 'top_k_values': top_k_values}
    _L1_ffn_all = _L1_ffn_setup()
    _L1_ffn_in = {k: v for k, v in _L1_ffn_all.items() if k in ('wi_w', 'wo_w', 'lora_As', 'lora_Bs', 'top_k_indices', 'top_k_values')}
    del _L1_ffn_all

    def _L2_xattn_setup():
        import jax, jax.numpy as jnp
        import numpy as np
        DIM = 256
        NUM_HEADS = 16
        DIM_HEAD = 64
        INNER = NUM_HEADS * DIM_HEAD
        SCALE = DIM_HEAD ** (-0.5)

        def _layernorm(x, gamma, beta, eps=1e-05):
            mu = jnp.mean(x, axis=-1, keepdims=True)
            var = jnp.mean(jnp.square(x - mu), axis=-1, keepdims=True)
            return (x - mu) * jax.lax.rsqrt(var + eps) * gamma + beta
        key = jax.random.key(seed)
        ks = jax.random.split(key, 8)
        B, SQ, SK = (2, 512, 1024)
        x = jax.random.normal(ks[0], (B, SQ, DIM), dtype=jnp.float32)
        context = jax.random.normal(ks[1], (B, SK, DIM), dtype=jnp.float32)
        ln_gamma = jnp.ones((DIM,), jnp.float32)
        ln_beta = jnp.zeros((DIM,), jnp.float32)
        w_q = jax.random.normal(ks[2], (DIM, INNER), dtype=jnp.float32) / np.sqrt(DIM)
        w_kv = jax.random.normal(ks[3], (DIM, 2 * INNER), dtype=jnp.float32) / np.sqrt(DIM)
        w_out = jax.random.normal(ks[4], (INNER, DIM), dtype=jnp.float32) / np.sqrt(INNER)
        b_out = jnp.zeros((DIM,), jnp.float32)
        gate = jnp.array([0.5], jnp.float32)
        return {'x': x, 'context': context, 'ln_gamma': ln_gamma, 'ln_beta': ln_beta, 'w_q': w_q, 'w_kv': w_kv, 'w_out': w_out, 'b_out': b_out, 'gate': gate}
    _L2_xattn_all = _L2_xattn_setup()
    _L2_xattn_in = {k: v for k, v in _L2_xattn_all.items() if k in ('ln_gamma', 'ln_beta', 'w_q', 'w_kv', 'w_out', 'b_out', 'gate')}
    del _L2_xattn_all

    def _L2_ffn_setup():
        import jax, jax.numpy as jnp
        import numpy as np
        B, S, H = (8, 256, 256)
        FF = 1024
        E = 8
        TOP_K = 2
        LN_EPS = 1e-12

        def _layernorm(x, w, b):
            mu = jnp.mean(x, axis=-1, keepdims=True)
            var = jnp.mean(jnp.square(x - mu), axis=-1, keepdims=True)
            return (x - mu) * jax.lax.rsqrt(var + LN_EPS) * w + b
        key = jax.random.key(seed)
        ks = jax.random.split(key, 8)
        sc_h = 1.0 / np.sqrt(H)
        sc_ff = 1.0 / np.sqrt(FF)
        return {'hidden_states': jax.random.normal(ks[0], (B, S, H), jnp.float32), 'router_w': jax.random.normal(ks[1], (E, H), jnp.float32) * sc_h, 'router_b': jnp.zeros((E,), jnp.float32), 'w1': jax.random.normal(ks[2], (E, FF, H), jnp.float32) * sc_h, 'b1': jax.random.normal(ks[3], (E, FF), jnp.float32) * 0.01, 'w2': jax.random.normal(ks[4], (E, H, FF), jnp.float32) * sc_ff, 'b2': jax.random.normal(ks[5], (E, H), jnp.float32) * 0.01, 'ln_w': jnp.ones((H,), jnp.float32), 'ln_b': jnp.zeros((H,), jnp.float32)}
    _L2_ffn_all = _L2_ffn_setup()
    _L2_ffn_in = {k: v for k, v in _L2_ffn_all.items() if k in ('router_w', 'router_b', 'w1', 'b1', 'w2', 'b2', 'ln_w', 'ln_b')}
    del _L2_ffn_all

    def _L3_xattn_setup():
        import jax, jax.numpy as jnp
        import numpy as np
        D_MODEL = 256
        NUM_HEADS = 16
        D_K = D_MODEL // NUM_HEADS
        key = jax.random.key(seed)
        ks = jax.random.split(key, 12)
        B, S = (2, 512)
        scale = 1.0 / np.sqrt(D_MODEL)
        inp = {'query': jax.random.normal(ks[0], (B, S, D_MODEL), jnp.float32), 'key': jax.random.normal(ks[1], (B, S, D_MODEL), jnp.float32), 'value': jax.random.normal(ks[2], (B, S, D_MODEL), jnp.float32), 'mask': jnp.ones((B, S, S), jnp.int32), 'Wq': jax.random.normal(ks[3], (D_MODEL, D_MODEL), jnp.float32) * scale, 'bq': jnp.zeros((D_MODEL,), jnp.float32), 'Wk': jax.random.normal(ks[4], (D_MODEL, D_MODEL), jnp.float32) * scale, 'bk': jnp.zeros((D_MODEL,), jnp.float32), 'Wv': jax.random.normal(ks[5], (D_MODEL, D_MODEL), jnp.float32) * scale, 'bv': jnp.zeros((D_MODEL,), jnp.float32), 'Wo': jax.random.normal(ks[6], (D_MODEL, D_MODEL), jnp.float32) * scale, 'bo': jnp.zeros((D_MODEL,), jnp.float32)}
        return inp
    _L3_xattn_all = _L3_xattn_setup()
    _L3_xattn_in = {k: v for k, v in _L3_xattn_all.items() if k in ('Wq', 'bq', 'Wk', 'bk', 'Wv', 'bv', 'Wo', 'bo')}
    del _L3_xattn_all

    def _L3_ffn_setup():
        import jax, jax.numpy as jnp
        import numpy as np
        B, S, D_MODEL, D_HIDDEN = (4, 512, 256, 1024)

        def act_quant(x):
            scale = 127.0 / jnp.clip(jnp.max(jnp.abs(x), axis=-1, keepdims=True), 1e-05)
            return jnp.clip(jnp.round(x * scale), -128, 127) / scale

        def weight_quant(w):
            scale = 1.0 / jnp.clip(jnp.mean(jnp.abs(w)), 1e-05)
            return jnp.clip(jnp.round(w * scale), -1, 1) / scale

        def bit_linear(x, w):
            xq = x + jax.lax.stop_gradient(act_quant(x) - x)
            wq = w + jax.lax.stop_gradient(weight_quant(w) - w)
            return jnp.einsum('bsd,hd->bsh', xq, wq)

        def depthwise_conv1d(x_bcl, w, b):
            y = jax.lax.conv_general_dilated(x_bcl, w, window_strides=(1,), padding=[(1, 1)], dimension_numbers=('NCH', 'OIH', 'NCH'), feature_group_count=x_bcl.shape[1])
            return y + b[None, :, None]
        key = jax.random.key(seed)
        ks = jax.random.split(key, 5)
        lim1 = 1.0 / np.sqrt(D_MODEL)
        lim2 = 1.0 / np.sqrt(D_HIDDEN)
        limc = 1.0 / np.sqrt(3.0)
        return {'x': jax.random.normal(ks[0], (B, S, D_MODEL), dtype=jnp.float32), 'w1': jax.random.uniform(ks[1], (D_HIDDEN, D_MODEL), jnp.float32, -lim1, lim1), 'conv_w': jax.random.uniform(ks[2], (D_HIDDEN, 1, 3), jnp.float32, -limc, limc), 'conv_b': jax.random.uniform(ks[3], (D_HIDDEN,), jnp.float32, -limc, limc), 'w2': jax.random.uniform(ks[4], (D_MODEL, D_HIDDEN), jnp.float32, -lim2, lim2)}
    _L3_ffn_all = _L3_ffn_setup()
    _L3_ffn_in = {k: v for k, v in _L3_ffn_all.items() if k in ('w1', 'conv_w', 'conv_b', 'w2')}
    del _L3_ffn_all
    return {'x': x, 'ctx_1024': ctx_1024, 'mask_Bx1xS2_bk0': mask_Bx1xS2_bk0, 'mask_BxSxS2_if1': mask_BxSxS2_if1, 'L0_xattn_Wq': _L0_xattn_in['Wq'], 'L0_xattn_Wk': _L0_xattn_in['Wk'], 'L0_xattn_Wv': _L0_xattn_in['Wv'], 'L0_xattn_Wp': _L0_xattn_in['Wp'], 'L0_xattn_focusing_factor': _L0_xattn_in['focusing_factor'], 'L0_ffn_ln_gamma': _L0_ffn_in['ln_gamma'], 'L0_ffn_ln_beta': _L0_ffn_in['ln_beta'], 'L0_ffn_router_w': _L0_ffn_in['router_w'], 'L0_ffn_w12': _L0_ffn_in['w12'], 'L0_ffn_w3': _L0_ffn_in['w3'], 'L1_xattn_W_out': _L1_xattn_in['W_out'], 'L1_xattn_scale': _L1_xattn_in['scale'], 'L1_xattn_log_C': _L1_xattn_in['log_C'], 'L1_ffn_wi_w': _L1_ffn_in['wi_w'], 'L1_ffn_wo_w': _L1_ffn_in['wo_w'], 'L1_ffn_lora_As': _L1_ffn_in['lora_As'], 'L1_ffn_lora_Bs': _L1_ffn_in['lora_Bs'], 'L1_ffn_top_k_indices': _L1_ffn_in['top_k_indices'], 'L1_ffn_top_k_values': _L1_ffn_in['top_k_values'], 'L2_xattn_ln_gamma': _L2_xattn_in['ln_gamma'], 'L2_xattn_ln_beta': _L2_xattn_in['ln_beta'], 'L2_xattn_w_q': _L2_xattn_in['w_q'], 'L2_xattn_w_kv': _L2_xattn_in['w_kv'], 'L2_xattn_w_out': _L2_xattn_in['w_out'], 'L2_xattn_b_out': _L2_xattn_in['b_out'], 'L2_xattn_gate': _L2_xattn_in['gate'], 'L2_ffn_router_w': _L2_ffn_in['router_w'], 'L2_ffn_router_b': _L2_ffn_in['router_b'], 'L2_ffn_w1': _L2_ffn_in['w1'], 'L2_ffn_b1': _L2_ffn_in['b1'], 'L2_ffn_w2': _L2_ffn_in['w2'], 'L2_ffn_b2': _L2_ffn_in['b2'], 'L2_ffn_ln_w': _L2_ffn_in['ln_w'], 'L2_ffn_ln_b': _L2_ffn_in['ln_b'], 'L3_xattn_Wq': _L3_xattn_in['Wq'], 'L3_xattn_bq': _L3_xattn_in['bq'], 'L3_xattn_Wk': _L3_xattn_in['Wk'], 'L3_xattn_bk': _L3_xattn_in['bk'], 'L3_xattn_Wv': _L3_xattn_in['Wv'], 'L3_xattn_bv': _L3_xattn_in['bv'], 'L3_xattn_Wo': _L3_xattn_in['Wo'], 'L3_xattn_bo': _L3_xattn_in['bo'], 'L3_ffn_w1': _L3_ffn_in['w1'], 'L3_ffn_conv_w': _L3_ffn_in['conv_w'], 'L3_ffn_conv_b': _L3_ffn_in['conv_b'], 'L3_ffn_w2': _L3_ffn_in['w2']}

def reference(x, ctx_1024, mask_Bx1xS2_bk0, mask_BxSxS2_if1, L0_xattn_Wq, L0_xattn_Wk, L0_xattn_Wv, L0_xattn_Wp, L0_xattn_focusing_factor, L0_ffn_ln_gamma, L0_ffn_ln_beta, L0_ffn_router_w, L0_ffn_w12, L0_ffn_w3, L1_xattn_W_out, L1_xattn_scale, L1_xattn_log_C, L1_ffn_wi_w, L1_ffn_wo_w, L1_ffn_lora_As, L1_ffn_lora_Bs, L1_ffn_top_k_indices, L1_ffn_top_k_values, L2_xattn_ln_gamma, L2_xattn_ln_beta, L2_xattn_w_q, L2_xattn_w_kv, L2_xattn_w_out, L2_xattn_b_out, L2_xattn_gate, L2_ffn_router_w, L2_ffn_router_b, L2_ffn_w1, L2_ffn_b1, L2_ffn_w2, L2_ffn_b2, L2_ffn_ln_w, L2_ffn_ln_b, L3_xattn_Wq, L3_xattn_bq, L3_xattn_Wk, L3_xattn_bk, L3_xattn_Wv, L3_xattn_bv, L3_xattn_Wo, L3_xattn_bo, L3_ffn_w1, L3_ffn_conv_w, L3_ffn_conv_b, L3_ffn_w2):
    import jax
    import jax.numpy as jnp

    def _L0_xattn_ref(q, k, v, Wq, Wk, Wv, Wp, focusing_factor):
        import jax, jax.numpy as jnp
        import numpy as np
        B, N, D = (4, 1024, 256)
        H = 16
        HD = D // H
        EPS = 1e-06
        BASE_SPARSITY = 0.3
        KEEP = max(int((1.0 - BASE_SPARSITY) * HD), 1)
        LEAKY_SLOPE = 0.01

        def _focus(x, focusing_factor):
            x = jnp.abs(jnp.where(x >= 0, x, LEAKY_SLOPE * x)) + EPS
            nrm = x.mean(axis=-1, keepdims=True)
            return jax.nn.softmax(jnp.log(x) * focusing_factor, axis=-1) * nrm

        def _to_heads(x):
            b, n, d = x.shape
            return x.reshape(b, n, H, HD).transpose(0, 2, 1, 3).reshape(b * H, n, HD)

        def _topk_sparsify(x):
            c = x.shape[-1]
            flat = x.reshape(-1, c)
            _, idx = jax.lax.top_k(jnp.abs(flat), KEEP)
            rows = jnp.arange(flat.shape[0])[:, None]
            mask = jnp.zeros(flat.shape, dtype=bool).at[rows, idx].set(True)
            return (flat * mask).reshape(x.shape)
        b, n, d = q.shape
        q = q @ Wq.T
        k = k @ Wk.T
        v = v @ Wv.T
        q = _focus(q, focusing_factor)
        k = _focus(k, focusing_factor)
        qh, kh, vh = (_to_heads(q), _to_heads(k), _to_heads(v))
        qh = _topk_sparsify(qh)
        kh = _topk_sparsify(kh)
        length_k = float(n)
        sqrt_l = jnp.sqrt(jnp.asarray(length_k, dtype=q.dtype))
        k_mean = kh.mean(axis=1)
        z_inv = jnp.einsum('bnd,bd->bn', qh, k_mean) + EPS
        kv = jnp.einsum('bnc,bnd->bcd', kh / sqrt_l, vh / sqrt_l)
        y = jnp.einsum('bnc,bcd->bnd', qh, kv) / z_inv[..., None]
        y = y.reshape(b, H, n, HD).transpose(0, 2, 1, 3).reshape(b, n, d)
        return y @ Wp.T

    def _L0_ffn_ref(x, ln_gamma, ln_beta, router_w, w12, w3):
        import math
        import jax, jax.numpy as jnp
        import numpy as np
        D_MODEL = 256
        D_FF = 1024
        E = 8
        K = 2
        CAP_FACTOR = 1.25
        CLAMP = 10000.0
        LN_EPS = 1e-05
        B, S = (2, 512)
        Bq, Sq, D = x.shape
        T = Bq * Sq
        mu = jnp.mean(x, axis=-1, keepdims=True)
        var = jnp.mean(jnp.square(x - mu), axis=-1, keepdims=True)
        xn = (x - mu) * jax.lax.rsqrt(var + LN_EPS) * ln_gamma + ln_beta
        xf = xn.reshape(T, D)
        logits = jnp.clip(xf @ router_w.T, -CLAMP, CLAMP)
        top_v, top_i = jax.lax.top_k(logits, K)
        m = jnp.max(top_v, axis=-1, keepdims=True)
        ev = jnp.exp(top_v - m)
        top_p = ev / (jnp.sum(ev, axis=-1, keepdims=True) + 1e-12)
        Stot = T * K
        experts = top_i.reshape(-1)
        weights = top_p.reshape(-1)
        tokens = jnp.repeat(jnp.arange(T), K)
        oh = (experts[:, None] == jnp.arange(E)[None, :]).astype(jnp.int32)
        pos = jnp.take_along_axis(jnp.cumsum(oh, axis=0) - 1, experts[:, None], axis=1)[:, 0]
        C = max(1, math.ceil(T * K * CAP_FACTOR / E))
        kept = pos < C
        slot = jnp.where(kept, experts * C + pos, E * C)
        buf = jnp.zeros((E * C + 1, D), x.dtype).at[slot].set(xf[tokens])
        xb = buf[:E * C].reshape(E, C, D)
        gu = jnp.einsum('ecd,efd->ecf', xb, w12)
        g, u = jnp.split(gu, 2, axis=-1)
        h = jax.nn.silu(g) * u
        yb = jnp.einsum('ecf,edf->ecd', h, w3).reshape(E * C, D)
        ys = yb[jnp.minimum(slot, E * C - 1)] * (weights * kept.astype(weights.dtype))[:, None]
        out = jnp.zeros((T, D), x.dtype).at[tokens].add(ys)
        return out.reshape(Bq, Sq, D)

    def _L1_xattn_ref(query, key, value, mask, W_out, scale, log_C):
        import jax, jax.numpy as jnp
        import numpy as np
        B, S, E, H = (4, 512, 256, 16)
        DH = E // H

        def _make_heads(v, n_heads):
            b, n, e = v.shape
            return jnp.moveaxis(v.reshape(b, n, n_heads, e // n_heads), -2, 0)
        q = _make_heads(query, H)
        k = _make_heads(key, H)
        v = _make_heads(value, H)
        d_k = q.shape[-1]
        u = jnp.einsum('hbqd,hbkd->hbqk', q, k) * scale / np.sqrt(d_k)
        logits = jnp.tanh(u) * jnp.exp(log_C)
        logits = jnp.where(mask, -jnp.inf, logits)
        attn = jax.nn.softmax(logits, axis=-1)
        out_heads = jnp.einsum('hbqk,hbkd->hbqd', attn, v)
        out = jnp.moveaxis(out_heads, 0, -2).reshape(query.shape)
        return out @ W_out.T

    def _L1_ffn_ref(hidden_states, wi_w, wo_w, lora_As, lora_Bs, top_k_indices, top_k_values):
        import jax, jax.numpy as jnp
        import numpy as np
        D_MODEL, D_FF, NUM_EXPERTS, RANK, TOP_K = (256, 1024, 8, 16, 2)
        B, S = (8, 512)

        def _expert_ffn(h, wi_w, wo_w, A, Bm):
            inter = jnp.einsum('bsd,fd->bsf', h, wi_w)
            lora = jnp.einsum('bsr,fr->bsf', jnp.einsum('bsd,rd->bsr', h, A), Bm)
            inter = jax.nn.relu(inter + lora)
            return jnp.einsum('bsf,df->bsd', inter, wo_w)
        out = jnp.zeros_like(hidden_states)
        for k in range(top_k_values.shape[0]):
            A = jnp.take(lora_As, top_k_indices[k], axis=0)
            Bm = jnp.take(lora_Bs, top_k_indices[k], axis=0)
            out = out + top_k_values[k] * _expert_ffn(hidden_states, wi_w, wo_w, A, Bm)
        return out

    def _L2_xattn_ref(x, context, ln_gamma, ln_beta, w_q, w_kv, w_out, b_out, gate):
        import jax, jax.numpy as jnp
        import numpy as np
        DIM = 256
        NUM_HEADS = 16
        DIM_HEAD = 64
        INNER = NUM_HEADS * DIM_HEAD
        SCALE = DIM_HEAD ** (-0.5)

        def _layernorm(x, gamma, beta, eps=1e-05):
            mu = jnp.mean(x, axis=-1, keepdims=True)
            var = jnp.mean(jnp.square(x - mu), axis=-1, keepdims=True)
            return (x - mu) * jax.lax.rsqrt(var + eps) * gamma + beta
        B, SQ, _ = x.shape
        SK = context.shape[1]
        xn = _layernorm(x, ln_gamma, ln_beta)
        q = (xn @ w_q).reshape(B, SQ, NUM_HEADS, DIM_HEAD)
        kv = context @ w_kv
        k, v = jnp.split(kv, 2, axis=-1)
        k = k.reshape(B, SK, NUM_HEADS, DIM_HEAD)
        v = v.reshape(B, SK, NUM_HEADS, DIM_HEAD)
        scores = jnp.einsum('bqhd,bkhd->bhqk', q * SCALE, k)
        attn = jax.nn.softmax(scores, axis=-1)
        out = jnp.einsum('bhqk,bkhd->bqhd', attn, v).reshape(B, SQ, INNER)
        out = out @ w_out + b_out
        return out * jnp.tanh(gate[0])

    def _L2_ffn_ref(hidden_states, router_w, router_b, w1, b1, w2, b2, ln_w, ln_b):
        import jax, jax.numpy as jnp
        import numpy as np
        B, S, H = (8, 256, 256)
        FF = 1024
        E = 8
        TOP_K = 2
        LN_EPS = 1e-12

        def _layernorm(x, w, b):
            mu = jnp.mean(x, axis=-1, keepdims=True)
            var = jnp.mean(jnp.square(x - mu), axis=-1, keepdims=True)
            return (x - mu) * jax.lax.rsqrt(var + LN_EPS) * w + b
        b, s, h = hidden_states.shape
        flat = hidden_states.reshape(-1, h)
        logits = flat @ router_w.T + router_b
        topk_vals, topk_idx = jax.lax.top_k(logits, TOP_K)
        topk_w = jax.nn.softmax(topk_vals, axis=-1)
        out = jnp.zeros_like(flat)
        n_exp = w1.shape[0]
        for e in range(n_exp):
            cw = jnp.sum(jnp.where(topk_idx == e, topk_w, 0.0), axis=-1)
            y = jax.nn.gelu(flat @ w1[e].T + b1[e], approximate=False)
            y = y @ w2[e].T + b2[e]
            out = out + y * cw[:, None]
        out = out.reshape(b, s, h) + hidden_states
        return _layernorm(out, ln_w, ln_b)

    def _L3_xattn_ref(query, key, value, mask, Wq, bq, Wk, bk, Wv, bv, Wo, bo):
        import jax, jax.numpy as jnp
        import numpy as np
        D_MODEL = 256
        NUM_HEADS = 16
        D_K = D_MODEL // NUM_HEADS
        B, S, _ = query.shape
        q = query @ Wq.T + bq
        k = key @ Wk.T + bk
        v = value @ Wv.T + bv
        q = q.reshape(B, S, NUM_HEADS, D_K).transpose(0, 2, 1, 3)
        k = k.reshape(B, -1, NUM_HEADS, D_K).transpose(0, 2, 1, 3)
        v = v.reshape(B, -1, NUM_HEADS, D_K).transpose(0, 2, 1, 3)
        scores = jnp.einsum('bhqd,bhkd->bhqk', q, k) / jnp.sqrt(jnp.float32(D_K))
        scores = jnp.where(mask[:, None, :, :] == 0, jnp.float32(-1000000000.0), scores)
        attn = jax.nn.softmax(scores, axis=-1)
        ctx = jnp.einsum('bhqk,bhkd->bhqd', attn, v)
        ctx = ctx.transpose(0, 2, 1, 3).reshape(B, S, D_MODEL)
        return ctx @ Wo.T + bo

    def _L3_ffn_ref(x, w1, conv_w, conv_b, w2):
        import jax, jax.numpy as jnp
        import numpy as np
        B, S, D_MODEL, D_HIDDEN = (4, 512, 256, 1024)

        def act_quant(x):
            scale = 127.0 / jnp.clip(jnp.max(jnp.abs(x), axis=-1, keepdims=True), 1e-05)
            return jnp.clip(jnp.round(x * scale), -128, 127) / scale

        def weight_quant(w):
            scale = 1.0 / jnp.clip(jnp.mean(jnp.abs(w)), 1e-05)
            return jnp.clip(jnp.round(w * scale), -1, 1) / scale

        def bit_linear(x, w):
            xq = x + jax.lax.stop_gradient(act_quant(x) - x)
            wq = w + jax.lax.stop_gradient(weight_quant(w) - w)
            return jnp.einsum('bsd,hd->bsh', xq, wq)

        def depthwise_conv1d(x_bcl, w, b):
            y = jax.lax.conv_general_dilated(x_bcl, w, window_strides=(1,), padding=[(1, 1)], dimension_numbers=('NCH', 'OIH', 'NCH'), feature_group_count=x_bcl.shape[1])
            return y + b[None, :, None]
        h = bit_linear(x, w1)
        h = depthwise_conv1d(h.transpose(0, 2, 1), conv_w, conv_b)
        h = h.transpose(0, 2, 1)
        h = jax.nn.silu(h)
        return bit_linear(h, w2)
    x = x + _L0_xattn_ref(_layernorm(x, axis=-1), ctx_1024, ctx_1024, L0_xattn_Wq, L0_xattn_Wk, L0_xattn_Wv, L0_xattn_Wp, L0_xattn_focusing_factor)
    x = x + _L0_ffn_ref(_layernorm(x, axis=-1), L0_ffn_ln_gamma, L0_ffn_ln_beta, L0_ffn_router_w, L0_ffn_w12, L0_ffn_w3)
    x = x + _L1_xattn_ref(_layernorm(x, axis=-1), ctx_1024, ctx_1024, mask_Bx1xS2_bk0, L1_xattn_W_out, L1_xattn_scale, L1_xattn_log_C)
    x = x + _L1_ffn_ref(_layernorm(x, axis=-1), L1_ffn_wi_w, L1_ffn_wo_w, L1_ffn_lora_As, L1_ffn_lora_Bs, L1_ffn_top_k_indices, L1_ffn_top_k_values)
    x = x + _L2_xattn_ref(_layernorm(x, axis=-1), ctx_1024, L2_xattn_ln_gamma, L2_xattn_ln_beta, L2_xattn_w_q, L2_xattn_w_kv, L2_xattn_w_out, L2_xattn_b_out, L2_xattn_gate)
    x = x + _L2_ffn_ref(_layernorm(x, axis=-1), L2_ffn_router_w, L2_ffn_router_b, L2_ffn_w1, L2_ffn_b1, L2_ffn_w2, L2_ffn_b2, L2_ffn_ln_w, L2_ffn_ln_b)
    x = x + _L3_xattn_ref(_layernorm(x, axis=-1), ctx_1024, ctx_1024, mask_BxSxS2_if1, L3_xattn_Wq, L3_xattn_bq, L3_xattn_Wk, L3_xattn_bk, L3_xattn_Wv, L3_xattn_bv, L3_xattn_Wo, L3_xattn_bo)
    x = x + _L3_ffn_ref(_layernorm(x, axis=-1), L3_ffn_w1, L3_ffn_conv_w, L3_ffn_conv_b, L3_ffn_w2)
    return x

_drawn_inputs = setup_inputs


def setup_inputs(seed=0):
    import zlib

    import numpy as np

    out = dict(_drawn_inputs(seed))
    spreads = {'L0_ffn_ln_gamma': (1.0, 0.2),
     'L0_ffn_ln_beta': (0.0, 0.1),
     'L2_xattn_ln_gamma': (1.0, 0.2),
     'L2_xattn_ln_beta': (0.0, 0.1),
     'L2_xattn_b_out': (0.0, 0.1),
     'L2_ffn_router_b': (0.0, 0.1),
     'L2_ffn_ln_w': (1.0, 0.2),
     'L2_ffn_ln_b': (0.0, 0.1),
     'L3_xattn_bq': (0.0, 0.1),
     'L3_xattn_bk': (0.0, 0.1),
     'L3_xattn_bv': (0.0, 0.1),
     'L3_xattn_bo': (0.0, 0.1)}
    factors = {}
    for name, (base, spread) in spreads.items():
        noise = np.random.default_rng([zlib.crc32(name.encode()), seed]).standard_normal(out[name].shape)
        drawn = base * np.exp(spread * noise) if base else spread * noise
        out[name] = jnp.asarray(drawn.astype(out[name].dtype))
    for name, factor in factors.items():
        out[name] = (out[name] * factor).astype(out[name].dtype)
    return out
```

```python
import numpy as np
from contextlib import ExitStack

import concourse.bass as bass
from concourse import mybir

F32 = mybir.dt.float32
BF16 = mybir.dt.bfloat16
I32 = mybir.dt.int32
U32 = mybir.dt.uint32
ALU = mybir.AluOpType
ACT = mybir.ActivationFunctionType
AX = mybir.AxisListType

NB, S, D = 16, 112, 256
SK, KT = 375, 3
KP = SK // KT
DC = D // 128
H = 16
DH = D // H
HG = H // DC
FF, FC = 1024, 8
E = 8
GROUPS, GB = 4, 4
GT = GB * S
EPS = 1e-5
LAYERS = (0, 1, 2, 3, 4, 5, 6, 7)


def after(eng, sem, count):
    if not isinstance(count, int) or count > 0:
        eng.wait_ge(sem, count)


class Chain:

    def __init__(self, eng, sem, base=0):
        self.eng, self.sem, self.base, self.n = eng, sem, base, 0

    def step(self, instruction):
        self.n += 1
        instruction.then_inc(self.sem, 1)
        return instruction

    def link(self, instruction):
        self.step(instruction)
        self.eng.wait_ge(self.sem, self.base + self.n)


def each_batch(eng, body):
    body(0, 0)
    body(1, 1)
    with eng.Fori(1, NB // 2 - 1) as i:
        body(2 * i, 0)
        body(2 * i + 1, 1)
    body(NB - 2, 0)
    body(NB - 1, 1)


class Core:

    def __init__(self, nc, ctx, ins):
        self.nc, self.ctx, self.ins = nc, ctx, ins
        self.put_done, self.stored, self.got_in = (
            {pre: [ctx.enter_context(nc.semaphore(f"{pre}_{name}{i}")) for i in range(n)]
             for pre in ("L0_ffn", "L2_ffn")} for name, n in (("put", 1), ("stored", 2), ("got", 4)))
        self.used = []
        self.x = self.sb(ctx, "x_sb", [S, NB, D])
        self.mv = self.sb(ctx, "mv", [S, NB, 2])
        self.st6 = self.sb(ctx, "st6", [S, 2, 6])
        self.xs = self.sb(ctx, "xs", [S, 2, D])
        self.mv1 = self.sb(ctx, "mv1", [S, 2, 2])
        self.st46 = self.sb(ctx, "st46", [S, 4, 6])
        self.mv4 = self.sb(ctx, "mv4", [S, 4, 2])
        self.mv2 = self.sb(ctx, "mv2", [S, NB, 2])
        self.tick = self.sb(ctx, "tick", [1, H])
        self.std = self.sb(ctx, "std", [S, NB])
        self.rstd = self.sb(ctx, "rstd", [S, NB])
        self.ident = self.sb(ctx, "ident", [128, 128])
        self.headmask = self.sb(ctx, "headmask", [128, HG])
        self.eps = self.sb(ctx, "eps", [128, 1])

    def sb(self, ctx, name, shape, dt=F32):
        return ctx.enter_context(self.nc.sbuf_tensor(name, shape, dt))

    KEEPS = 3

    def keep(self, ch, dve, b, h):
        ch.link(dve.bn_stats(self.st6[:, h, :], self.xs[:, h, :]))
        dve.tensor_scalar(self.x[:, b, :], self.xs[:, h, :], 1.0, None, ALU.mult)
        ch.link(dve.bn_aggr(self.mv1[:, h, :], self.st6[:, h, :]))
        ch.step(dve.tensor_scalar(self.mv[:, b, :], self.mv1[:, h, :], 1.0, None, ALU.mult))

    def banks(self, ctx, name, n):
        return ctx.enter_context(self.nc.psum_tensor(name, [128, n, 512], F32))

    def sem(self, ctx, name):
        s = ctx.enter_context(self.nc.semaphore(name))
        self.used.append(s.num)
        return s

    def clear(self):
        self.nc.all_engine_barrier(sems_to_clear=range(min(self.used), max(self.used) + 1))
        self.used = []


def load_inputs(core):
    nc, ins = core.nc, core.ins
    with ExitStack() as ctx:
        x_in = core.sem(ctx, "in_x")
        const_in = core.sem(ctx, "in_const")
        chain = core.sem(ctx, "in_chain")
        with nc.Block() as block:
            @block.sync
            def _(sp):
                sp.dma_start(core.x[:, :, :], ins["x"].rearrange("b s d -> s b d")).then_inc(x_in, 16)
                sp.dma_start(core.ident[:, :], ins["ident"]).then_inc(const_in, 16)
                sp.dma_start(core.headmask[:, :], ins["headmask"]).then_inc(const_in, 16)
                sp.wait_ge(const_in, 32)

            @block.vector
            def _(dve):
                ch = Chain(dve, chain)
                ch.step(dve.memset(core.eps[:, :], EPS))
                dve.wait_ge(x_in, 16)
                for b in range(NB):
                    ch.link(dve.bn_stats(core.st6[:, b % 2, :], core.x[:, b, :]))
                    ch.step(dve.bn_aggr(core.mv[:, b, :], core.st6[:, b % 2, :]))


def store_output(core, out):
    nc = core.nc
    with ExitStack() as ctx:
        stored = core.sem(ctx, "out_stored")
        with nc.Block() as block:
            @block.sync
            def _(sp):
                sp.dma_start(out.rearrange("b s d -> s b d"), core.x[:, :, :]).then_inc(stored, 16)
                sp.wait_ge(stored, 16)


def focused_attention(core):
    nc, ins = core.nc, core.ins
    x, ident = core.x, core.ident
    KEEP = max(int((1.0 - 0.3) * DH), 1)
    DROP = DH - KEEP
    TILES = KT + 1
    KV = 128 + HG
    TINY = 1e-6
    with ExitStack() as ctx:
        def sb(name, shape, dt=F32):
            return core.sb(ctx, "fa_" + name, shape, dt)

        def sem(name):
            return core.sem(ctx, "fa_" + name)

        wq, wk, wv, wp = (sb(n, [128, DC, D]) for n in ("wq", "wk", "wv", "wp"))
        focus = sb("focus", [128, 1])
        tag = sb("tag", [KP, D], U32)
        kvmask = sb("kvmask", [128, KV])
        tiny = sb("tiny", [128, 1])
        ones = sb("ones", [KP, HG])
        xn = sb("xn", [S, 2, D])
        xt = sb("xt", [128, 2, DC, KP])
        ctxT = sb("ctxT", [128, 2, DC, SK])
        rows = sb("rows", [KP, 3, KT, D])
        w = sb("w", [KP, 2, TILES, D])
        asum, tmax, ntmax, esum, cw = (sb(n, [KP, 2, TILES]) for n in ("asum", "tmax", "ntmax", "esum", "cw"))
        keys = sb("keys", [KP, TILES, D])
        top = sb("top", [KP, TILES * H, 8])
        kh = sb("kh", [KP, 2, TILES, D])
        gt = sb("gt", [128, DC, D])
        kv = sb("kv", [128, DC, KV])
        qT = sb("qT", [128, DC, S])
        zr = sb("zr", [S, DC, HG])
        yn = sb("yn", [S, D])
        yT = sb("yT", [128, DC, S])
        pre_ps = [core.banks(ctx, f"fa_pre{i}", 2) for i in range(2)]
        xt_ps, g_ps, kv_ps, fin_ps = (core.banks(ctx, "fa_" + n, 1) for n in ("xt_ps", "g_ps", "kv_ps", "fin_ps"))
        fin_y = g_ps

        w_in, ctx_in = sem("w_in"), [sem("c0"), sem("c1")]
        rows_in = [sem(f"r{i}") for i in range(2)]
        std_done, setup, chain = sem("std"), sem("setup"), sem("chain")
        xn_done, x_out, x_done, pre_out, pre_done = (sem(n) for n in ("xn", "x_out", "x", "pre_out", "pre"))
        leaky_done, ln_done, t_done, exp_done, kh_done = (sem(n) for n in ("leaky", "ln", "t", "exp", "kh"))
        g_out, g_done, kv_out, kv_done, q_out, q_done = (sem(n) for n in ("g_out", "g", "kv_out", "kv", "q_out", "q"))
        y_out, y_done, yT_out, yT_done, p_out, p_done = (sem(n) for n in ("y_out", "y", "yT_out", "yT", "p_out", "p"))
        NLOADS = 7

        def holds(b, low, high=NB - 1):
            return not isinstance(b, int) or low <= b <= high

        with nc.Block() as block:
            @block.sync
            def _(sp):
                for to, src in ((wq, "Wq"), (wk, "Wk"), (wv, "Wv"), (wp, "Wp")):
                    sp.dma_start(to[:, :, :], ins["L0_xattn_" + src]).then_inc(w_in, 16)
                sp.dma_start(focus[:, :], ins["L0_xattn_focus"].partition_broadcast(128)).then_inc(w_in, 16)
                sp.dma_start(tag[:, :], ins["tag"].partition_broadcast(KP)).then_inc(w_in, 16)
                sp.dma_start(kvmask[:, :], ins["kvmask"]).then_inc(w_in, 16)

                def load(b, h):
                    after(sp, pre_out, b - 1)
                    sp.dma_start(ctxT[:, h, :, :], ins["ctxT"][b]).then_inc(ctx_in[h], 16)
                    after(sp, g_out, b - 1)
                    sp.dma_start(rows[:, h, :, :], ins["ctx_rows"][b]).then_inc(rows_in[h], 16)
                each_batch(sp, load)

            @block.gpsimd
            def _(pool):
                pool.memset(xt[:, :, :, :], 0.0).then_inc(setup, 1)
                pool.memset(tiny[:, :], TINY).then_inc(setup, 1)
                pool.memset(ones[:, :], 1.0).then_inc(setup, 1)

            @block.scalar
            def _(act):
                act.activation(core.std[:, :], core.mv[:, :, 1], ACT.Sqrt, bias=core.eps[0:S, :]).then_inc(std_done, 1)
                act.wait_ge(setup, 3)

                def project_done(b, h):
                    act.wait_ge(x_out, b + 1)
                    after(act, pre_out, b - 1)
                    act.activation(xt[:, h, :, 0:S], xt_ps[:, 0, 0:DC * S].rearrange("p (c s) -> p c s", c=DC),
                                   ACT.Copy).then_inc(x_done, 1)
                    act.wait_ge(pre_out, b + 1)
                    after(act, kh_done, b - 1)
                    act.activation(w[:, h, :, :].rearrange("p (a t) d -> p a (t d)", a=2), pre_ps[h][0:KP, :, :],
                                   ACT.Copy).then_inc(pre_done, 1)

                def take_yT(b):
                    act.wait_ge(yT_out, b + 1)
                    after(act, p_out, b)
                    act.activation(yT[:, :, :], fin_ps[:, 0, 0:DC * S].rearrange("p (c s) -> p c s", c=DC),
                                   ACT.Copy).then_inc(yT_done, 1)

                def log(b, h):
                    act.wait_ge(leaky_done, b + 1)
                    act.activation(w[:, h, :, :], w[:, h, :, :], ACT.Ln, bias=tiny[0:KP, :]).then_inc(ln_done, 1)

                def exp(b, h):
                    act.wait_ge(t_done, b + 1)
                    for t in range(TILES):
                        r = act.activation(w[:, h, t, :], w[:, h, t, :], ACT.Exp, bias=ntmax[:, h, t:t + 1],
                                           accum_out=esum[:, h, t:t + 1])
                    r.then_inc(exp_done, 1)

                def body(b, h):
                    if holds(b, 1):
                        act.wait_ge(g_out, b)
                        after(act, kv_out, b - 1)
                        act.activation(gt[:, :, :].rearrange("p c d -> p (c d)"), g_ps[:, 0, :], ACT.Copy).then_inc(g_done, 1)
                        act.wait_ge(q_out, b)
                        act.activation(qT[:, :, :], xt_ps[:, 0, DC * S:2 * DC * S].rearrange(
                            "p (c s) -> p c s", c=DC), ACT.Copy).then_inc(q_done, 1)
                    if holds(b, 2):
                        take_yT(b - 2)
                    if holds(b, 0, NB - 2):
                        log(b + 1, 1 - h)
                    if holds(b, 0, NB - 2):
                        exp(b + 1, 1 - h)
                    if holds(b, 0, NB - 3):
                        project_done(b + 2, h)
                project_done(0, 0)
                project_done(1, 1)
                log(0, 0)
                exp(0, 0)
                each_batch(act, body)
                take_yT(NB - 2)
                act.wait_ge(g_out, NB)
                act.activation(gt[:, :, :].rearrange("p c d -> p (c d)"), g_ps[:, 0, :], ACT.Copy).then_inc(g_done, 1)
                act.wait_ge(q_out, NB)
                act.activation(qT[:, :, :], xt_ps[:, 0, DC * S:2 * DC * S].rearrange("p (c s) -> p c s", c=DC),
                               ACT.Copy).then_inc(q_done, 1)
                take_yT(NB - 1)

            @block.vector
            def _(dve):
                ch = Chain(dve, chain)
                dve.wait_ge(std_done, 1)
                ch.link(dve.reciprocal(core.rstd[:, :], core.std[:, :]))
                start = ch.n
                dve.wait_ge(w_in, NLOADS * 16)

                def normalize(b, h):
                    after(dve, x_out, b - 1)
                    dve.tensor_scalar(xn[:, h, :], x[:, b, :], core.mv[:, b, 0:1], core.rstd[:, bass.ts(b, 1)],
                                      ALU.subtract, ALU.mult).then_inc(xn_done, 1)

                def leaky(b, h):
                    dve.wait_ge(pre_done, b + 1)
                    for t in range(TILES):
                        r = dve.scalar_tensor_tensor(out=w[:, h, t, :], in0=w[:, h, t, :], scalar=-0.01, in1=w[:, h, t, :],
                                                     op0=ALU.mult, op1=ALU.max, accum_out=asum[:, h, t:t + 1])
                    r.then_inc(leaky_done, 1)

                def exponents(b, h, c):
                    dve.wait_ge(ln_done, b + 1)
                    for t in range(TILES):
                        c.step(dve.tensor_scalar(w[:, h, t, :], w[:, h, t, :], focus[0:KP, :], -3e38, ALU.mult, ALU.max,
                                                 accum_out=tmax[:, h, t:t + 1]))
                    dve.wait_ge(c.sem, c.base + c.n)
                    dve.tensor_scalar(ntmax[:, h, :], tmax[:, h, :], -1.0, None, ALU.mult).then_inc(t_done, 1)

                def rank(b, h, c):
                    dve.wait_ge(exp_done, b + 1)
                    c.link(dve.scalar_tensor_tensor(
                        out=keys[:, :, :].bitcast(U32), in0=w[:, h, :, :].bitcast(U32), scalar=0xFFFFFFF0,
                        in1=tag[:, :].unsqueeze(1).broadcast_to([KP, TILES, D]),
                        op0=ALU.bitwise_and, op1=ALU.bitwise_or))
                    dve.memset(core.tick[:, 0:1], 0.0)
                    for n in range(TILES * H):
                        r = dve.max(top[:, n, :], keys[:, n // H, (n % H) * DH:(n % H + 1) * DH])
                    c.step(r)

                def select(b, h, c):
                    dve.wait_ge(c.sem, c.base + c.n)
                    c.step(dve.tensor_tensor(keys[:, :, :].rearrange("p t (h d) -> p (t h) d", h=H),
                                             keys[:, :, :].rearrange("p t (h d) -> p (t h) d", h=H),
                                             top[:, :, DROP - 1:DROP].broadcast_to([KP, TILES * H, DH]), ALU.is_lt))
                    c.step(dve.reciprocal(cw[:, h, :], esum[:, h, :]))
                    c.link(dve.tensor_scalar(asum[:, h, :], asum[:, h, :], 1.0 / D, TINY, ALU.mult, ALU.add))
                    c.link(dve.tensor_tensor(cw[:, h, :], cw[:, h, :], asum[:, h, :], ALU.mult))
                    after(dve, q_out, b - 1)
                    after(dve, kv_out, b - 1)
                    for t in range(TILES):
                        r = dve.scalar_tensor_tensor(out=kh[:, h, t, :], in0=w[:, h, t, :], scalar=cw[:, h, t:t + 1],
                                                     in1=keys[:, t, :], op0=ALU.mult, op1=ALU.mult)
                    r.then_inc(kh_done, 1)

                def blocks(b):
                    dve.wait_ge(kv_out, b + 1)
                    after(dve, y_out, b)
                    dve.tensor_tensor(kv[:, :, :], kv_ps[:, 0, 0:DC * KV].rearrange("p (c k) -> p c k", c=DC),
                                      kvmask[:, :].unsqueeze(1).broadcast_to([128, DC, KV]), ALU.mult).then_inc(kv_done, 1)

                def head_mean(b, c):
                    dve.wait_ge(y_out, b + 1)
                    y = fin_y[0:S, 0, 0:DC * KV].rearrange("p (c k) -> p c k", c=DC)
                    c.link(dve.tensor_scalar(zr[:, :, :], y[:, :, 128:KV], TINY, None, ALU.add))
                    c.link(dve.reciprocal(zr[:, :, :], zr[:, :, :]))
                    after(dve, yT_out, b)
                    for g in range(DC):
                        r = dve.tensor_tensor(yn[:, g * 128:(g + 1) * 128].rearrange("p (h d) -> p h d", d=DH),
                                              y[:, g, 0:128].rearrange("p (h d) -> p h d", d=DH),
                                              zr[:, g, :].unsqueeze(2).broadcast_to([S, HG, DH]), ALU.mult)
                    r.then_inc(y_done, 1)

                def residual(b, h, c):
                    dve.wait_ge(p_out, b + 1)
                    dve.tensor_tensor(core.xs[:, h, :], fin_ps[0:S, 0, 0:D], x[:, b, :], ALU.add).then_inc(p_done, 1)
                    dve.wait_ge(p_done, b + 1)
                    core.keep(c, dve, b, h)

                PER = (TILES) + 2 + 4 + 2 + core.KEEPS

                def body(b, h):
                    c = Chain(dve, chain, base_of(b))
                    if holds(b, 0, NB - 3):
                        normalize(b + 2, h)
                    rank(b, h, c)
                    if holds(b, 0, NB - 2):
                        leaky(b + 1, 1 - h)
                    if holds(b, 1):
                        blocks(b - 1)
                    select(b, h, c)
                    if holds(b, 2):
                        residual(b - 2, h, c)
                    if holds(b, 0, NB - 2):
                        exponents(b + 1, 1 - h, c)
                    if holds(b, 1):
                        head_mean(b - 1, c)
                    if isinstance(b, int):
                        done_steps[b] = c.n
                    else:
                        assert c.n == PER

                done_steps = {}
                FIRST = [2 + 4 + TILES, 2 + 4 + TILES + 2]

                def base_of(b):
                    if isinstance(b, int) and b < 2:
                        return start + before + sum(FIRST[:b])
                    return start + before + sum(FIRST) + (b - 2) * PER
                normalize(0, 0)
                normalize(1, 1)
                leaky(0, 0)
                c = Chain(dve, chain, start)
                exponents(0, 0, c)
                before = c.n
                each_batch(dve, body)
                assert [done_steps[0], done_steps[1]] == FIRST and done_steps[NB - 2] == PER
                c = Chain(dve, chain, base_of(NB - 1) + done_steps[NB - 1])
                residual(NB - 2, 0, c)
                blocks(NB - 1)
                head_mean(NB - 1, c)
                residual(NB - 1, 1, c)

            @block.tensor
            def _(pe):
                def project(b, h):
                    pe.wait_ge(xn_done, b + 1)
                    after(pe, x_done, b)
                    for c in range(DC):
                        m = pe.transpose(xt_ps[:, 0, c * S:(c + 1) * S], xn[:, h, c * 128:(c + 1) * 128], ident[0:S, 0:S])
                    m.then_inc(x_out, 1)
                    pe.wait_ge(ctx_in[h], (b - h) * 8 + 16)
                    after(pe, pre_done, b - 1)
                    for t in range(KT):
                        for c in range(DC):
                            pe.matmul(pre_ps[h][0:KP, t // 2, (t % 2) * D:(t % 2 + 1) * D],
                                      ctxT[:, h, c, t * KP:(t + 1) * KP], wk[:, c, :], start=(c == 0), stop=(c == DC - 1))
                    pe.wait_ge(x_done, b + 1)
                    for c in range(DC):
                        m = pe.matmul(pre_ps[h][0:KP, 1, D:2 * D], xt[:, h, c, :], wq[:, c, :],
                                      start=(c == 0), stop=(c == DC - 1))
                    m.then_inc(pre_out, 1)

                def products(b, h):
                    pe.wait_ge(kh_done, b + 1)
                    pe.wait_ge(rows_in[h], (b - h) * 8 + 16)
                    after(pe, y_done, b)
                    for c in range(DC):
                        for t in range(KT):
                            m = pe.matmul(g_ps[:, 0, c * D:(c + 1) * D], rows[:, h, t, c * 128:(c + 1) * 128],
                                          kh[:, h, t, :], start=(t == 0), stop=(t == KT - 1))
                    m.then_inc(g_out, 1)
                    after(pe, q_done, b)
                    for c in range(DC):
                        m = pe.transpose(xt_ps[:, 0, (DC + c) * S:(DC + c + 1) * S], kh[0:S, h, KT, c * 128:(c + 1) * 128],
                                         ident[0:S, 0:S])
                    m.then_inc(q_out, 1)
                    after(pe, kv_done, b)
                    for g in range(DC):
                        for t in range(KT):
                            pe.matmul(kv_ps[:, 0, g * KV + 128:(g + 1) * KV], kh[:, h, t, g * 128:(g + 1) * 128],
                                      ones[:, :], start=(t == 0), stop=(t == KT - 1))
                    pe.wait_ge(g_done, b + 1)
                    for g in range(DC):
                        for c in range(DC):
                            m = pe.matmul(kv_ps[:, 0, g * KV:g * KV + 128], gt[:, c, g * 128:(g + 1) * 128],
                                          wv[:, c, g * 128:(g + 1) * 128], start=(c == 0), stop=(c == DC - 1))
                    m.then_inc(kv_out, 1)

                def attend(b):
                    pe.wait_ge(q_done, b + 1)
                    pe.wait_ge(kv_done, b + 1)
                    for g in range(DC):
                        m = pe.matmul(fin_y[0:S, 0, g * KV:(g + 1) * KV], qT[:, g, :], kv[:, g, :], start=True, stop=True)
                    m.then_inc(y_out, 1)

                def finish(b):
                    pe.wait_ge(y_done, b + 1)
                    after(pe, p_done, b)
                    for c in range(DC):
                        m = pe.transpose(fin_ps[:, 0, c * S:(c + 1) * S], yn[:, c * 128:(c + 1) * 128], ident[0:S, 0:S])
                    m.then_inc(yT_out, 1)
                    pe.wait_ge(yT_done, b + 1)
                    for c in range(DC):
                        m = pe.matmul(fin_ps[0:S, 0, 0:D], yT[:, c, :], wp[:, c, :], start=(c == 0), stop=(c == DC - 1))
                    m.then_inc(p_out, 1)

                def body(b, h):
                    if holds(b, 1):
                        products(b - 1, 1 - h)
                    if holds(b, 2):
                        finish(b - 2)
                    if holds(b, 1):
                        attend(b - 1)
                    if holds(b, 0, NB - 3):
                        project(b + 2, h)
                pe.wait_ge(w_in, NLOADS * 16)
                pe.wait_ge(setup, 3)
                project(0, 0)
                project(1, 1)
                each_batch(pe, body)
                finish(NB - 2)
                products(NB - 1, 1)
                attend(NB - 1)
                finish(NB - 1)


def tanh_attention(core):
    nc, ins = core.nc, core.ins
    x, mv, rstd, ident = core.x, core.mv, core.rstd, core.ident
    CH = DC * KT
    with ExitStack() as ctx:
        def sb(name, shape, dt=F32):
            return core.sb(ctx, "ta_" + name, shape, dt)

        def sem(name):
            return core.sem(ctx, "ta_" + name)

        wo = sb("wo", [128, DC, D])
        par = sb("par", [128, 2])
        tscale, cap = sb("tscale", [128, 1]), sb("cap", [128, 1])
        msk = sb("msk", [KP, NB, KT], mybir.dt.uint8)
        hide = sb("hide", [KP, NB, KT])
        hide_b = sb("hide_b", [KP, 2, KT])
        xn = sb("xn", [S, 2, D])
        xt = sb("xt", [128, 2, DC, S])
        qbd = sb("qbd", [128, 2, DC, HG, S])
        kT = sb("kT", [128, 2, DC, SK])
        ctxr = sb("ctxr", [KP, 2, KT, D])
        vaug = sb("vaug", [KP, 2, KT, H, DH + 1])
        pT = sb("pT", [KP, 2, DC, KT, HG * S])
        rec = sb("rec", [S, H])
        on = sb("on", [S, 2, D])
        onT = sb("onT", [128, 2, DC, S])
        xt_ps = core.banks(ctx, "ta_xt_ps", 1)
        fin_ps = core.banks(ctx, "ta_fin_ps", 1)
        s_ps = [core.banks(ctx, f"ta_s_ps{i}", 2) for i in range(2)]
        o_ps = [core.banks(ctx, f"ta_o_ps{i}", 1) for i in range(2)]

        w_in, ctx_in = sem("w_in"), [sem("ctx_in0"), sem("ctx_in1")]
        std_done, rstd_done, cap_done, setup = sem("std"), sem("rstd"), sem("cap"), sem("setup")
        chain = sem("chain")
        xn_done, xt_out, xt_done, q_done, v_done = (sem(n) for n in ("xn", "xt_out", "xt", "q", "v"))
        s_out, tanh_done, exp_done = sem("s_out"), sem("tanh"), sem("exp")
        pv_out, on_done, onT_out, onT_done, y_out, y_done = (
            sem(n) for n in ("pv_out", "on", "onT_out", "onT", "y_out", "y"))
        PER = 1 + core.KEEPS

        with nc.Block() as block:
            @block.sync
            def _(sp):
                sp.dma_start(par[:, 0:1], ins["L1_xattn_scale"].partition_broadcast(128)).then_inc(w_in, 16)
                sp.dma_start(par[:, 1:2], ins["L1_xattn_log_C"].partition_broadcast(128)).then_inc(w_in, 16)
                sp.dma_start(msk[:, :, :], ins["key_mask"]).then_inc(w_in, 16)
                sp.dma_start(wo[:, :, :], ins["L1_xattn_W_outT"]).then_inc(w_in, 16)

                def load(b, h):
                    after(sp, s_out, (b - 1) * CH)
                    after(sp, v_done, b - 1)
                    sp.dma_start(kT[:, h, :, :], ins["ctxT"][b]).then_inc(ctx_in[h], 16)
                    sp.dma_start(ctxr[:, h, :, :], ins["ctx_rows"][b]).then_inc(ctx_in[h], 16)
                each_batch(sp, load)

            @block.gpsimd
            def _(pool):
                pool.memset(vaug[:, :, :, :, DH:DH + 1], 1.0).then_inc(setup, 1)
                pool.wait_ge(w_in, 64)
                pool.tensor_scalar(hide[:, :, :], msk[:, :, :], -1e30, None, ALU.mult).then_inc(setup, 1)
                pool.wait_ge(setup, 2)

                def body(b, h):
                    after(pool, exp_done, (b - 1) * CH)
                    pool.wait_ge(xt_done, b + 1)
                    after(pool, s_out, (b - 1) * CH)
                    for c in range(DC):
                        q = pool.tensor_tensor(
                            qbd[:, h, c, :, :], xt[:, h, c, :].unsqueeze(1).broadcast_to([128, HG, S]),
                            core.headmask[:, :].unsqueeze(2).broadcast_to([128, HG, S]), ALU.mult)
                    q.then_inc(q_done, 1)
                    pool.wait_ge(ctx_in[h], 16 * (b - h) + 32)
                    after(pool, pv_out, 2 * (b - 1))
                    pool.tensor_copy(hide_b[:, h, :], hide[:, b, :])
                    pool.tensor_copy(vaug[:, h, :, :, 0:DH],
                                     ctxr[:, h, :, :].rearrange("p k (h d) -> p k h d", h=H)).then_inc(v_done, 1)
                each_batch(pool, body)

            @block.scalar
            def _(act):
                act.activation(core.std[:, :], mv[:, :, 1], ACT.Sqrt, bias=core.eps[0:S, :]).then_inc(std_done, 1)
                act.wait_ge(w_in, 64)
                act.activation(cap[:, :], par[:, 1:2], ACT.Exp).then_inc(cap_done, 1)
                act.activation(tscale[:, :], par[:, 0:1], ACT.Copy, scale=1.0 / np.sqrt(DH)).then_inc(cap_done, 1)
                act.wait_ge(cap_done, 2)

                def exponentials(b, h, c):
                    act.wait_ge(tanh_done, b * CH + c + 1)
                    act.wait_ge(v_done, b + 1)
                    p = pT[:, h, c // KT, c % KT, :]
                    act.activation(p, p, ACT.Exp, bias=hide_b[:, h, c % KT:c % KT + 1],
                                   scale=cap[0:KP, :]).then_inc(exp_done, 1)

                def body(b, h):
                    for c in range(CH):
                        act.wait_ge(s_out, b * CH + c + 1)
                        after(act, pv_out, 2 * (b - 2) + c // KT + 1)
                        act.activation(pT[:, h, c // KT, c % KT, :].rearrange("p (j n) -> p j n", j=2),
                                       s_ps[c % 2][0:KP, :, 0:GT], ACT.Tanh,
                                       scale=tscale[0:KP, :]).then_inc(tanh_done, 1)
                        if c:
                            exponentials(b, h, c - 1)
                        elif not isinstance(b, int) or b > 0:
                            exponentials(b - 1, 1 - h, CH - 1)
                each_batch(act, body)
                exponentials(NB - 1, 1, CH - 1)

            @block.vector
            def _(dve):
                dve.wait_ge(std_done, 1)
                dve.reciprocal(rstd[:, :], core.std[:, :]).then_inc(rstd_done, 1)
                dve.wait_ge(rstd_done, 1)

                def normalize(b, h):
                    after(dve, xt_out, b - 1)
                    dve.tensor_scalar(xn[:, h, :], x[:, b, :], mv[:, b, 0:1], rstd[:, bass.ts(b, 1)],
                                      ALU.subtract, ALU.mult).then_inc(xn_done, 1)

                def take_xt(b, h):
                    dve.wait_ge(xt_out, b + 1)
                    after(dve, q_done, b - 1)
                    dve.tensor_copy(xt[:, h, :, :], xt_ps[:, 0, 0:DC * S].rearrange(
                        "p (c s) -> p c s", c=DC)).then_inc(xt_done, 1)

                def head_mean(b, h, ch):
                    dve.wait_ge(pv_out, 2 * b + 2)
                    o = o_ps[h][0:S, 0, 0:H * (DH + 1)].rearrange("p (h d) -> p h d", h=H)
                    ch.link(dve.reciprocal(rec[:, :], o[:, :, DH]))
                    after(dve, onT_out, b - 1)
                    dve.tensor_tensor(on[:, h, :].rearrange("p (h d) -> p h d", h=H), o[:, :, 0:DH],
                                      rec[:, :].unsqueeze(2).broadcast_to([S, H, DH]), ALU.mult).then_inc(on_done, 1)

                def finish(b, h, ch):
                    dve.wait_ge(onT_out, b + 1)
                    after(dve, y_out, b - 1)
                    dve.tensor_copy(onT[:, h, :, :], fin_ps[:, 0, 0:DC * S].rearrange(
                        "p (c s) -> p c s", c=DC)).then_inc(onT_done, 1)
                    dve.wait_ge(y_out, b + 1)
                    dve.tensor_tensor(core.xs[:, h, :], fin_ps[0:S, 0, 0:D], x[:, b, :],
                                      ALU.add).then_inc(y_done, 1)
                    dve.wait_ge(y_done, b + 1)
                    core.keep(ch, dve, b, h)

                def body(b, h):
                    if not isinstance(b, int) or b < NB - 1:
                        normalize(b + 1, 1 - h)
                    first = isinstance(b, int) and b == 0
                    ch = Chain(dve, chain, (b - 1) * PER)
                    if not first:
                        head_mean(b - 1, 1 - h, ch)
                    if not isinstance(b, int) or b < NB - 1:
                        take_xt(b + 1, 1 - h)
                    if not first:
                        finish(b - 1, 1 - h, ch)
                normalize(0, 0)
                take_xt(0, 0)
                each_batch(dve, body)
                ch = Chain(dve, chain, (NB - 1) * PER)
                head_mean(NB - 1, 1, ch)
                finish(NB - 1, 1, ch)

            @block.tensor
            def _(pe):
                def transpose_x(b, h):
                    pe.wait_ge(xn_done, b + 1)
                    after(pe, xt_done, b)
                    for c in range(DC):
                        t = pe.transpose(xt_ps[:, 0, c * S:(c + 1) * S], xn[:, h, c * 128:(c + 1) * 128],
                                         ident[0:S, 0:S])
                    t.then_inc(xt_out, 1)

                def scores(b, h, c):
                    g, kt = c // KT, c % KT
                    after(pe, tanh_done, b * CH + c - 1)
                    for j in range(2):
                        m = pe.matmul(s_ps[c % 2][0:KP, j, 0:GT], kT[:, h, g, kt * KP:(kt + 1) * KP],
                                      qbd[:, h, g, 4 * j:4 * j + 4, :], start=True, stop=True)
                    m.then_inc(s_out, 1)

                def products(b, h, g, part):
                    if part == 0:
                        pe.wait_ge(exp_done, b * CH + (g + 1) * KT)
                        pe.wait_ge(v_done, b + 1)
                        if g == 0:
                            after(pe, on_done, b - 1)
                    for hh in range(part * HG // 2, (part + 1) * HG // 2):
                        head = g * HG + hh
                        for kt in range(KT):
                            m = pe.matmul(o_ps[h][0:S, 0, head * (DH + 1):(head + 1) * (DH + 1)],
                                          pT[:, h, g, kt, hh * S:(hh + 1) * S], vaug[:, h, kt, head, :],
                                          start=(kt == 0), stop=(kt == KT - 1))
                    if part == 1:
                        m.then_inc(pv_out, 1)

                def transpose_o(b, h):
                    pe.wait_ge(on_done, b + 1)
                    after(pe, y_done, b)
                    for c in range(DC):
                        t = pe.transpose(fin_ps[:, 0, c * S:(c + 1) * S], on[:, h, c * 128:(c + 1) * 128],
                                         ident[0:S, 0:S])
                    t.then_inc(onT_out, 1)

                def project(b, h):
                    pe.wait_ge(onT_done, b + 1)
                    for c in range(DC):
                        m = pe.matmul(fin_ps[0:S, 0, 0:D], onT[:, h, c, :], wo[:, c, :],
                                      start=(c == 0), stop=(c == DC - 1))
                    m.then_inc(y_out, 1)

                def body(b, h):
                    first = isinstance(b, int) and b == 0
                    last = isinstance(b, int) and b == NB - 1
                    pe.wait_ge(ctx_in[h], 16 * (b - h) + 32)
                    pe.wait_ge(q_done, b + 1)
                    scores(b, h, 0)
                    scores(b, h, 1)
                    if not first:
                        products(b - 1, 1 - h, 1, 0)
                    scores(b, h, 2)
                    if not first:
                        products(b - 1, 1 - h, 1, 1)
                    if not last:
                        transpose_x(b + 1, 1 - h)
                    scores(b, h, 3)
                    if not first:
                        transpose_o(b - 1, 1 - h)
                    scores(b, h, 4)
                    products(b, h, 0, 0)
                    if not first:
                        project(b - 1, 1 - h)
                    scores(b, h, 5)
                    products(b, h, 0, 1)
                transpose_x(0, 0)
                pe.wait_ge(w_in, 64)
                each_batch(pe, body)
                products(NB - 1, 1, 1, 0)
                products(NB - 1, 1, 1, 1)
                transpose_o(NB - 1, 1)
                project(NB - 1, 1)


def second_statistics(core, dve, ch, xn4, std_done):
    T = 4
    per = 3 * T + 1
    with dve.Fori(0, NB // T) as i:
        c = Chain(dve, ch.sem, ch.base + ch.n + i * per)
        for t in range(T):
            c.step(dve.tensor_scalar(xn4[:, t, :], core.x[:, T * i + t, :], core.mv[:, T * i + t, 0:1],
                                     core.rstd[:, bass.ts(T * i + t, 1)], ALU.subtract, ALU.mult))
        dve.wait_ge(c.sem, c.base + c.n)
        for t in range(T):
            c.step(dve.bn_stats(core.st46[:, t, :], xn4[:, t, :]))
        dve.wait_ge(c.sem, c.base + c.n)
        dve.memset(core.tick[:, 0:1], 0.0)
        for t in range(T):
            c.step(dve.bn_aggr(core.mv4[:, t, :], core.st46[:, t, :]))
        dve.wait_ge(c.sem, c.base + c.n)
        c.link(dve.tensor_scalar(core.mv2[:, bass.ts(i, T), :], core.mv4[:, :, :], 1.0, None, ALU.mult))
        assert c.n == per
    ch.n += per * (NB // T)
    dve.sem_inc(std_done, 1)


def softmax_attention(core, pre, wide):
    nc, ins = core.nc, core.ins
    x, ident = core.x, core.ident
    dh = 64 if wide else DH
    inner = H * dh
    IC = inner // 128
    AV = dh if wide else dh + 1
    QB = min(IC, 4)
    VW = 512 if wide else D
    NK, NQ, NO = IC, IC // QB, IC // QB
    v_parts = [[(kt, w)] for kt in range(KT) for w in range(inner // VW)] if wide else [[(0, 0), (1, 0)], [(2, 0)]]
    NV = len(v_parts)
    K, Q, V, O = ([(kind, i) for i in range(n)] for kind, n in (("k", NK), ("q", NQ), ("v", NV), ("o", NO)))
    X, Y = ("x", 0), ("y", 0)
    if wide:
        slots = [[K[0]], [K[1]], [K[2], K[3]], [K[4]], [K[5]], [O[0]], [O[1], K[6]], [K[7]], [Y], [Q[0]], [Q[1]],
                 [V[0]], [V[1], V[2]], [V[3]], [V[4], V[5]], [X]]
    else:
        slots = [[K[0]], [], [K[1]], [], [Q[0]], [], [O[0]], [], [Y], [], [V[0]], [], [V[1]], [], [X], []]
    order = [j for jobs in slots for j in jobs]
    LT = 2 if wide else 3
    LP = LT + 1
    J = len(order)
    assert J % 2 == 0
    with ExitStack() as ctx:
        n_ = pre + "_"

        def sb(name, shape, dt=F32):
            return core.sb(ctx, n_ + name, shape, dt)

        def sem(name):
            return core.sem(ctx, n_ + name)

        wq, wk = sb("wq", [128, DC, inner]), sb("wk", [128, DC, inner])
        wv, wo = sb("wv", [128, DC, inner]), sb("wo", [128, IC, D])
        bias_y = sb("bias_y", [S, D])
        if wide:
            gb = sb("gb", [128, 2, DC])
            gate = sb("gate", [128, 2])
            xn4 = sb("xn4", [S, 4, D])
            std2, rstd2 = sb("std2", [S, NB]), sb("rstd2", [S, NB])
            sums = sb("sums", [S, 2, H])
        else:
            bq, bqs, bk = sb("bq", [128, DC]), sb("bqs", [128, DC]), sb("bk", [128, DC])
            bv = sb("bv", [S, D])
            msk = sb("msk", [S, 2, SK], I32)
            hide = sb("hide", [S, 2, SK])
            ssb = sb("ssb", [S, 4, SK])
            qbd = sb("qbd", [128, 2, DC, HG, S])
        xn1, xn = sb("xn1", [S, D]), sb("xn", [S, 2, D])
        xt = sb("xt", [128, 2, DC, S])
        ctxT = sb("ctxT", [128, 2, DC, SK])
        qt = sb("qt", [128, 2, IC, S])
        kt_sb = sb("kt", [128, 2, IC, SK])
        v_sb = sb("v", [KP, 2, KT, H, AV])
        least = sb("least", [S, 2, H])
        p_sb = sb("p", [S, 4, SK])
        pt_sb = sb("pt", [KP, 4, KT, S])
        rec = sb("rec", [S, H])
        on = sb("on", [S, inner])
        onT = sb("onT", [128, IC, S])
        job_ps = [core.banks(ctx, f"{n_}job{i}", 1) for i in range(2)]
        s_ps = [core.banks(ctx, f"{n_}s{i}", 1) for i in range(2)]
        pt_ps = [core.banks(ctx, f"{n_}pt{i}", 1) for i in range(2)]
        o_ps = core.banks(ctx, n_ + "o", 2)

        w_in, ctx_in, std_done, setup, chain = sem("w_in"), [sem("c0"), sem("c1")], sem("std"), sem("setup"), sem("chain")
        out = {t: sem(t + "_out") for t in "kqvxoy"}
        done = {t: sem(t + "_done") for t in "kqvxoy"}
        xn_done, q_ready, mask_done = sem("xn"), sem("q_ready"), sem("mask")
        s_out, low_done, exp_done = sem("s_out"), sem("low"), sem("exp")
        t_out, pt_done, pv_out, on_done = sem("t_out"), sem("pt"), sem("pv"), sem("on")
        per_batch = {"k": NK, "q": NQ, "v": NV, "x": 1, "o": NO, "y": 1}

        def made(kind, b, i=0):
            return b * per_batch[kind] + i + 1

        def exists(b):
            return not isinstance(b, int) or 0 <= b < NB

        OF = {"x": 2, "k": 1, "q": 1, "v": 1, "o": -1, "y": -1}

        def wait_bank(pe, kind, i, turn):
            at = order.index((kind, i)) - 2
            while True:
                if at < 0:
                    at, turn = at + J, turn - 1
                if isinstance(turn, int) and turn < -2:
                    return
                k, n = order[at]
                if exists(turn + OF[k]):
                    break
                at -= 2
            after(pe, done[k], made(k, turn + OF[k], n))

        def behind(b, head, lag):
            return (b, head - lag) if head >= lag else (b - 1, H + head - lag)

        def projections(run):
            run("x", 0, -2, 0, 0)
            for kind, i in K + Q + V:
                run(kind, i, -1, 0, 0)
            run("x", 0, -1, 1, 1)

        def slot_jobs(run, b, h, head, kinds):
            for kind, i in slots[head]:
                of = b + OF[kind]
                if kind in kinds and exists(of):
                    run(kind, i, b, of, (h + OF[kind]) % 2)

        with nc.Block() as block:
            @block.sync
            def _(sp):
                loads = [(wq[:, :, :], ins[pre + "_Wq"]), (wk[:, :, :], ins[pre + "_Wk"]),
                         (wv[:, :, :], ins[pre + "_Wv"]), (wo[:, :, :], ins[pre + "_Wo"]),
                         (bias_y[:, :], ins[pre + "_bo"].partition_broadcast(S))]
                if wide:
                    loads += [(gb[:, 0, :], ins[pre + "_gamma"]), (gb[:, 1, :], ins[pre + "_beta"]),
                              (gate[:, 0:1], ins["L2_xattn_gate"].partition_broadcast(128))]
                else:
                    loads += [(bq[:, :], ins[pre + "_bq"]), (bk[:, :], ins[pre + "_bk"]),
                              (bv[:, :], ins[pre + "_bv"].partition_broadcast(S))]
                for to, src in loads:
                    sp.dma_start(to, src).then_inc(w_in, 16)

                def load(b, h):
                    after(sp, out["v"], (b - 1) * NV)
                    sp.dma_start(ctxT[:, h, :, :], ins["ctxT"][b]).then_inc(ctx_in[h], 16)
                    if not wide:
                        after(sp, mask_done, b - 1)
                        sp.dma_start(msk[:, h, :], ins["mask"][b]).then_inc(ctx_in[h], 16)
                each_batch(sp, load)
            CTX = 16 if wide else 32
            NLOADS = 8

            def wait_ctx(eng, b, h):
                eng.wait_ge(ctx_in[h], (b - h) * (CTX // 2) + CTX)

            @block.gpsimd
            def _(pool):
                if wide:
                    return
                pool.memset(v_sb[:, :, :, :, dh:AV], 1.0).then_inc(setup, 1)

                def body(b, h):
                    wait_ctx(pool, b, h)
                    after(pool, low_done, (b - 1) * H)
                    pool.wait_ge(done["q"], made("q", b))
                    after(pool, s_out, (b - 1) * H)
                    for c in range(DC):
                        q = pool.tensor_tensor(
                            qbd[:, h, c, :, :], qt[:, h, c, :].unsqueeze(1).broadcast_to([128, HG, S]),
                            core.headmask[:, :].unsqueeze(2).broadcast_to([128, HG, S]), ALU.mult)
                    q.then_inc(q_ready, 1)
                    pool.tensor_scalar(hide[:, h, :], msk[:, h, :], 0.0, 1e9, ALU.is_equal, ALU.mult).then_inc(mask_done, 1)
                each_batch(pool, body)

            @block.scalar
            def _(act):
                act.activation(core.std[:, :], core.mv[:, :, 1], ACT.Sqrt, bias=core.eps[0:S, :]).then_inc(std_done, 1)
                act.wait_ge(w_in, NLOADS * 16)
                if wide:
                    act.wait_ge(std_done, 2)
                    act.activation(std2[:, :], core.mv2[:, :, 1], ACT.Sqrt, bias=core.eps[0:S, :]).then_inc(std_done, 1)
                    act.activation(gate[:, 1:2], gate[:, 0:1], ACT.Tanh).then_inc(setup, 1)
                else:
                    act.activation(bqs[:, :], bq[:, :], ACT.Copy, scale=-dh ** -0.5).then_inc(setup, 1)
                    act.wait_ge(setup, 2)

                def job(kind, i, turn, b, h):
                    act.wait_ge(out[kind], made(kind, b, i))
                    ps = job_ps[order.index((kind, i)) % 2]
                    if kind == "k":
                        after(act, s_out, (b - 1) * H)
                        to, src = kt_sb[:, h, i, :], ps[:, 0, 0:SK]
                        if wide:
                            r = act.activation(to, src, ACT.Copy)
                        else:
                            r = act.activation(to, src, ACT.Identity, bias=bk[:, i:i + 1])
                    elif kind == "q":
                        after(act, s_out if wide else q_ready, (b - 1) * (H if wide else 1))
                        if wide:
                            r = act.activation(qt[:, h, i * QB:(i + 1) * QB, :],
                                               ps[:, 0, 0:QB * S].rearrange("p (c s) -> p c s", c=QB),
                                               ACT.Copy, scale=-dh ** -0.5)
                        else:
                            for c in range(DC):
                                r = act.activation(qt[:, h, c, :], ps[:, 0, c * S:(c + 1) * S], ACT.Identity,
                                                   bias=bqs[:, c:c + 1], scale=-dh ** -0.5)
                    elif kind == "v":
                        after(act, pv_out, (b - 1) * H)
                        for n, (kt, w) in enumerate(v_parts[i]):
                            hs = VW // dh
                            r = act.activation(v_sb[:, h, kt, w * hs:(w + 1) * hs, 0:dh],
                                               ps[0:KP, 0, n * VW:(n + 1) * VW].rearrange("p (h d) -> p h d", h=hs),
                                               ACT.Copy)
                    elif kind == "x":
                        after(act, out["v"], (b - 1) * NV)
                        for c in range(DC):
                            if wide:
                                r = act.activation(xt[:, h, c, :], ps[:, 0, c * S:(c + 1) * S], ACT.Identity,
                                                   bias=gb[:, 1, c:c + 1], scale=gb[:, 0, c:c + 1])
                            else:
                                r = act.activation(xt[:, h, c, :], ps[:, 0, c * S:(c + 1) * S], ACT.Copy)
                    elif kind == "o":
                        after(act, out["y"], b)
                        r = act.activation(onT[:, i * QB:(i + 1) * QB, :],
                                           ps[:, 0, 0:QB * S].rearrange("p (c s) -> p c s", c=QB), ACT.Copy)
                    r.then_inc(done[kind], 1)

                def exponential(b, h, head):
                    act.wait_ge(low_done, b * H + head + 1)
                    after(act, t_out, b * H + head - 3)
                    src = s_ps[head % 2][0:S, 0, 0:SK] if wide else ssb[:, head % 4, :]
                    more = dict(accum_out=sums[:, h, head:head + 1]) if wide else {}
                    act.activation(p_sb[:, head % 4, :], src, ACT.Exp, bias=least[:, h, head:head + 1],
                                   scale=-1.0, **more).then_inc(exp_done, 1)

                def body(b, h):
                    for head in range(H):
                        exponential(b, h, head)
                        slot_jobs(job, b, h, head, "kqvxo")
                projections(job)
                each_batch(act, body)
                for kind, i in O:
                    job(kind, i, NB, NB - 1, 1)

            @block.vector
            def _(dve):
                ch = Chain(dve, chain)
                dve.wait_ge(std_done, 1)
                ch.link(dve.reciprocal(core.rstd[:, :], core.std[:, :]))
                if wide:
                    second_statistics(core, dve, ch, xn4, std_done)
                    dve.wait_ge(std_done, 3)
                    ch.link(dve.reciprocal(rstd2[:, :], std2[:, :]))
                    dve.wait_ge(w_in, NLOADS * 16)
                    dve.wait_ge(setup, 1)
                    ch.link(dve.tensor_scalar(bias_y[:, :], bias_y[:, :], gate[0:S, 1:2], None, ALU.mult))
                else:
                    dve.wait_ge(w_in, NLOADS * 16)
                start = ch.n

                def normalize(b, h):
                    after(dve, out["x"], b - 1)
                    if wide:
                        after(dve, xn_done, 2 * b)
                        dve.tensor_scalar(xn1[:, :], x[:, b, :], core.mv[:, b, 0:1], core.rstd[:, bass.ts(b, 1)],
                                          ALU.subtract, ALU.mult).then_inc(xn_done, 1)
                        dve.wait_ge(xn_done, 2 * b + 1)
                        dve.tensor_scalar(xn[:, h, :], xn1[:, :], core.mv2[:, b, 0:1], rstd2[:, bass.ts(b, 1)],
                                          ALU.subtract, ALU.mult).then_inc(xn_done, 1)
                    else:
                        dve.tensor_scalar(xn[:, h, :], x[:, b, :], core.mv[:, b, 0:1], core.rstd[:, bass.ts(b, 1)],
                                          ALU.subtract, ALU.mult).then_inc(xn_done, 1)

                def lowest(b, h, head):
                    dve.wait_ge(s_out, b * H + head + 1)
                    s = s_ps[head % 2][0:S, 0, 0:SK]
                    low = least[:, h, head:head + 1]
                    if wide:
                        dve.tensor_reduce(low, s, AX.X, ALU.min).then_inc(low_done, 1)
                    else:
                        if head == 0:
                            dve.wait_ge(mask_done, b + 1)
                        after(dve, exp_done, b * H + head - 3)
                        dve.memset(core.tick[:, head:head + 1], 0.0)
                        dve.tensor_tensor_reduce(out=ssb[:, head % 4, :], in0=s, in1=hide[:, h, :], scale=1.0,
                                                 scalar=3e38, op0=ALU.add, op1=ALU.min,
                                                 accum_out=low).then_inc(low_done, 1)

                def take_pt(b, h, head):
                    dve.wait_ge(t_out, b * H + head + 1)
                    after(dve, pv_out, b * H + head - 3)
                    dve.tensor_copy(pt_sb[:, head % 4, :, :], pt_ps[head % 2][0:KP, 0, 0:KT * S].rearrange(
                        "p (k s) -> p k s", k=KT)).then_inc(pt_done, 1)

                def head_mean(b, h, w, ch):
                    dve.wait_ge(pv_out, b * H + 8 * w + 8)
                    o = o_ps[0:S, w, 0:8 * AV].rearrange("p (h d) -> p h d", h=8)
                    r8, on8 = rec[:, 8 * w:8 * w + 8], on[:, w * 8 * dh:(w + 1) * 8 * dh]
                    ch.link(dve.reciprocal(r8, sums[:, h, 8 * w:8 * w + 8] if wide else o[:, :, dh]))
                    after(dve, out["o"], b * NO)
                    r = dve.tensor_tensor(on8.rearrange("p (h d) -> p h d", h=8), o[:, :, 0:dh],
                                          r8.unsqueeze(2).broadcast_to([S, 8, dh]), ALU.mult)
                    if not wide:
                        ch.link(r)
                        r = dve.tensor_tensor(on8, on8, bv[:, w * 8 * dh:(w + 1) * 8 * dh], ALU.add)
                    r.then_inc(on_done, 1)

                def residual(b, h, ch):
                    dve.wait_ge(out["y"], b + 1)
                    y = job_ps[order.index(Y) % 2][0:S, 0, 0:D]
                    if wide:
                        r = dve.scalar_tensor_tensor(out=core.xs[:, h, :], in0=y, scalar=gate[0:S, 1:2],
                                                     in1=bias_y[:, :], op0=ALU.mult, op1=ALU.add)
                    else:
                        r = dve.tensor_tensor(core.xs[:, h, :], y, bias_y[:, :], ALU.add)
                    r.then_inc(done["y"], 1)
                    dve.wait_ge(done["y"], b + 1)
                    ch.link(dve.tensor_tensor(core.xs[:, h, :], core.xs[:, h, :], x[:, b, :], ALU.add))
                    core.keep(ch, dve, b, h)

                HALF = 1 if wide else 2
                PERB = 2 * HALF + 1 + core.KEEPS

                def body(b, h):
                    opening = isinstance(b, int) and b == 0
                    c = Chain(dve, chain, start if opening else start + HALF + (b - 1) * PERB)
                    for head in range(H):
                        lowest(b, h, head)
                        at, t = behind(b, head, LT)
                        if exists(at):
                            take_pt(at, h if head >= LT else 1 - h, t)
                        if head == LP and not opening:
                            head_mean(b - 1, 1 - h, 1, c)
                        if head == 9 and not opening:
                            residual(b - 1, 1 - h, c)
                        if head == 8 + LP:
                            head_mean(b, h, 0, c)
                        if head == 13 and exists(b + 2):
                            normalize(b + 2, h)
                    assert c.n == (HALF if opening else PERB)
                normalize(0, 0)
                normalize(1, 1)
                each_batch(dve, body)
                for head in range(LT):
                    take_pt(NB - 1, 1, H + head - LT)
                c = Chain(dve, chain, start + HALF + (NB - 1) * PERB)
                head_mean(NB - 1, 1, 1, c)
                residual(NB - 1, 1, c)

            @block.tensor
            def _(pe):
                def job(kind, i, turn, b, h):
                    wait_bank(pe, kind, i, turn)
                    ps = job_ps[order.index((kind, i)) % 2]
                    if kind == "k":
                        pe.wait_ge(done["x"], b + 1)
                        wait_ctx(pe, b, h)
                        for c in range(DC):
                            m = pe.matmul(ps[:, 0, 0:SK], wk[:, c, i * 128:(i + 1) * 128], ctxT[:, h, c, :],
                                          start=(c == 0), stop=(c == DC - 1))
                    elif kind == "q":
                        for n in range(QB):
                            for c in range(DC):
                                at = (i * QB + n) * 128
                                m = pe.matmul(ps[:, 0, n * S:(n + 1) * S], wq[:, c, at:at + 128], xt[:, h, c, :],
                                              start=(c == 0), stop=(c == DC - 1))
                    elif kind == "v":
                        for n, (kt, w) in enumerate(v_parts[i]):
                            for c in range(DC):
                                m = pe.matmul(ps[0:KP, 0, n * VW:(n + 1) * VW],
                                              ctxT[:, h, c, kt * KP:(kt + 1) * KP], wv[:, c, w * VW:(w + 1) * VW],
                                              start=(c == 0), stop=(c == DC - 1))
                    elif kind == "x":
                        pe.wait_ge(xn_done, (2 if wide else 1) * (b + 1))
                        for c in range(DC):
                            m = pe.transpose(ps[:, 0, c * S:(c + 1) * S], xn[:, h, c * 128:(c + 1) * 128],
                                             ident[0:S, 0:S])
                    elif kind == "o":
                        pe.wait_ge(on_done, 2 * b + (i + 1 if wide else 2))
                        for n in range(QB):
                            at = (i * QB + n) * 128
                            m = pe.transpose(ps[:, 0, n * S:(n + 1) * S], on[:, at:at + 128], ident[0:S, 0:S])
                    elif kind == "y":
                        pe.wait_ge(done["o"], made("o", b, NO - 1))
                        for c in range(IC):
                            m = pe.matmul(ps[0:S, 0, 0:D], onT[:, c, :], wo[:, c, :], start=(c == 0), stop=(c == IC - 1))
                    m.then_inc(out[kind], 1)

                def scores(b, h, head):
                    if head == 0:
                        pe.wait_ge(done["k"], made("k", b, NK - 1))
                        if wide:
                            pe.wait_ge(done["q"], made("q", b, NQ - 1))
                        else:
                            pe.wait_ge(q_ready, b + 1)
                    after(pe, exp_done if wide else low_done, b * H + head - 1)
                    if wide:
                        r = slice(64 * (head % 2), 64 * (head % 2) + 64)
                        q, k = qt[r, h, head // 2, :], kt_sb[r, h, head // 2, :]
                    else:
                        q, k = qbd[:, h, head // HG, head % HG, :], kt_sb[:, h, head // HG, :]
                    pe.matmul(s_ps[head % 2][0:S, 0, 0:SK], q, k, start=True, stop=True).then_inc(s_out, 1)

                def turn_p(b, h, head):
                    pe.wait_ge(exp_done, b * H + head + 1)
                    after(pe, pt_done, b * H + head - 1)
                    for kt in range(KT):
                        m = pe.transpose(pt_ps[head % 2][0:KP, 0, kt * S:(kt + 1) * S],
                                         p_sb[:, head % 4, kt * KP:(kt + 1) * KP], ident[0:S, 0:S])
                    m.then_inc(t_out, 1)

                def products(b, h, head):
                    pe.wait_ge(pt_done, b * H + head + 1)
                    if head == 0:
                        pe.wait_ge(done["v"], made("v", b, NV - 1))
                    if head % 8 == 0:
                        after(pe, on_done, 2 * b - 1 + head // 8)
                    o = o_ps[0:S, head // 8, (head % 8) * AV:(head % 8 + 1) * AV]
                    for kt in range(KT):
                        m = pe.matmul(o, pt_sb[:, head % 4, kt, :], v_sb[:, h, kt, head, :],
                                      start=(kt == 0), stop=(kt == KT - 1))
                    m.then_inc(pv_out, 1)

                def trail(b, h, head):
                    for lag, step in ((LT, turn_p), (LP, products)):
                        at, t = behind(b, head, lag)
                        if exists(at):
                            step(at, h if head >= lag else 1 - h, t)

                def body(b, h):
                    for head in range(H):
                        scores(b, h, head)
                        trail(b, h, head)
                        slot_jobs(job, b, h, head, "kqvxoy")
                pe.wait_ge(w_in, NLOADS * 16)
                pe.wait_ge(xn_done, 1)
                projections(job)
                each_batch(pe, body)
                for head in range(LP):
                    if head < LT:
                        turn_p(NB - 1, 1, H + head - LT)
                    products(NB - 1, 1, H + head - LP)
                for kind, i in O + [Y]:
                    job(kind, i, NB, NB - 1, 1)


def shared_experts(core):
    nc, ins = core.nc, core.ins
    x, ident = core.x, core.ident
    K = 2
    RING = 4
    with ExitStack() as ctx:
        def sb(name, shape, dt=F32):
            return core.sb(ctx, "se_" + name, shape, dt)

        def sem(name):
            return core.sem(ctx, "se_" + name)

        wi, wo = sb("wi", [128, DC, FF]), sb("wo", [128, FC, D])
        A, B = sb("A", [128, D]), sb("B", [128, FF])
        AK = sb("AK", [128, K, D])
        rank_expert = sb("rank_expert", [128, 1])
        chosen, chosen_f, sel = sb("chosen", [128, K], I32), sb("chosen_f", [128, K]), sb("sel", [128, K])
        val = sb("val", [128, K])
        W = sb("W", [128, K, DC, FF])
        xn = sb("xn", [S, 2, D])
        xnT = sb("xnT", [128, DC, NB * S])
        r0, r1 = sb("r0", [128, 2, GT]), sb("r1", [128, 2, GT])
        hT = sb("hT", [128, RING, GT])
        up_ps = [[core.banks(ctx, f"se_up{i}{k}", 1) for k in range(K)] for i in range(2)]
        dn_ps = [core.banks(ctx, f"se_dn{t}", 1) for t in range(GB)]
        w_in, std_done, ak_done, lora_out, lora_done = (sem(n) for n in ("w_in", "std", "ak", "lora_out", "lora"))
        xn_done, x_out, x_done = sem("xn"), sem("x_out"), sem("x")
        up_out, r0_done, r1_done, h_done, dn_step, dn_out, dn_done = (
            sem(n) for n in ("up_out", "r0", "r1", "h", "dn_step", "dn_out", "dn"))
        chain = sem("chain")

        with nc.Block() as block:
            @block.sync
            def _(sp):
                for to, src in ((A[:, :], ins["L1_ffn_A"]), (B[:, :], ins["L1_ffn_B"]),
                                (rank_expert[:, :], ins["rank_expert"]),
                                (chosen[:, :], ins["L1_ffn_chosen"].partition_broadcast(128)),
                                (val[:, :], ins["L1_ffn_values"].partition_broadcast(128)),
                                (wi[:, :, :], ins["L1_ffn_wi"]), (wo[:, :, :], ins["L1_ffn_wo"])):
                    sp.dma_start(to, src).then_inc(w_in, 16)

            @block.scalar
            def _(act):
                act.activation(core.std[:, :], core.mv[:, :, 1], ACT.Sqrt, bias=core.eps[0:S, :]).then_inc(std_done, 1)
                with act.Fori(0, GROUPS) as g:
                    for f in range(FC):
                        act.wait_ge(up_out, g * FC + f + 1)
                        after(act, h_done, g * FC + f - 1) if f >= 2 else act.wait_ge(h_done, g * FC)
                        act.activation(r1[:, f % 2, :], up_ps[f % 2][1][:, 0, 0:GT], ACT.Relu).then_inc(r1_done, 1)

            @block.vector
            def _(dve):
                ch = Chain(dve, chain)
                dve.wait_ge(w_in, 7 * 16)
                ch.link(dve.tensor_copy(chosen_f[:, :], chosen[:, :]))
                ch.link(dve.tensor_scalar(sel[:, :], chosen_f[:, :], rank_expert[:, :], None, ALU.is_equal))
                for k in range(K):
                    dve.tensor_scalar(AK[:, k, :], A[:, :], sel[:, k:k + 1], None, ALU.mult).then_inc(ak_done, 1)
                dve.wait_ge(std_done, 1)
                ch.link(dve.reciprocal(core.rstd[:, :], core.std[:, :]))
                n = 0
                for k in range(K):
                    for c in range(DC):
                        dve.wait_ge(lora_out, n // 2 + 1)
                        for half in range(2):
                            dve.tensor_tensor(W[:, k, c, half * 512:(half + 1) * 512], up_ps[n // 2 % 2][half][:, 0, :],
                                              wi[:, c, half * 512:(half + 1) * 512], ALU.add).then_inc(lora_done, 1)
                            n += 1

                def normalize(b, h):
                    after(dve, x_out, b - 1)
                    dve.tensor_scalar(xn[:, h, :], x[:, b, :], core.mv[:, b, 0:1], core.rstd[:, bass.ts(b, 1)],
                                      ALU.subtract, ALU.mult).then_inc(xn_done, 1)

                def spread(b, h):
                    if not isinstance(b, int) or b < NB - 1:
                        normalize(b + 1, 1 - h)
                    dve.wait_ge(x_out, b + 1)
                    dve.tensor_scalar(xnT[:, :, bass.ts(b, S)], dn_ps[h][:, 0, 0:DC * S].rearrange(
                        "p (c s) -> p c s", c=DC), 1.0, None, ALU.mult).then_inc(x_done, 1)
                normalize(0, 0)
                each_batch(dve, spread)

                start = ch.n
                PER = GB * core.KEEPS
                with dve.Fori(0, GROUPS) as g:
                    c = Chain(dve, chain, start + g * PER)
                    for f in range(FC):
                        dve.wait_ge(up_out, g * FC + f + 1)
                        dve.tensor_scalar(r0[:, f % 2, :], up_ps[f % 2][0][:, 0, 0:GT], 0.0, val[:, 0:1],
                                          ALU.max, ALU.mult).then_inc(r0_done, 1)
                        dve.wait_ge(r0_done, g * FC + f + 1)
                        dve.wait_ge(r1_done, g * FC + f + 1)
                        after(dve, dn_step, g * FC + f - RING + 1) if f >= RING else dve.wait_ge(dn_step, g * FC)
                        dve.scalar_tensor_tensor(out=hT[:, f % RING, :], in0=r1[:, f % 2, :], scalar=val[:, 1:2],
                                                 in1=r0[:, f % 2, :], op0=ALU.mult, op1=ALU.add).then_inc(h_done, 1)
                    dve.wait_ge(dn_step, (g + 1) * FC)
                    for t in range(GB):
                        b = GB * g + t
                        dve.tensor_tensor(core.xs[:, t % 2, :], dn_ps[t][0:S, 0, 0:D], x[:, b, :], ALU.add).then_inc(dn_done, 1)
                        dve.wait_ge(dn_done, g * GB + t + 1)
                        core.keep(c, dve, b, t % 2)
                    assert c.n == PER

            @block.tensor
            def _(pe):
                pe.wait_ge(w_in, 7 * 16)
                n = 0
                for k in range(K):
                    pe.wait_ge(ak_done, k + 1)
                    for c in range(DC):
                        after(pe, lora_done, 2 * (n - 1))
                        for half in range(2):
                            m = pe.matmul(up_ps[n % 2][half][:, 0, :], AK[:, k, c * 128:(c + 1) * 128],
                                          B[:, half * 512:(half + 1) * 512], start=True, stop=True)
                        m.then_inc(lora_out, 1)
                        n += 1

                def turn(b, h):
                    pe.wait_ge(xn_done, b + 1)
                    after(pe, x_done, b - 1)
                    for c in range(DC):
                        m = pe.transpose(dn_ps[h][:, 0, c * S:(c + 1) * S], xn[:, h, c * 128:(c + 1) * 128], ident[0:S, 0:S])
                    m.then_inc(x_out, 1)
                each_batch(pe, turn)
                pe.wait_ge(x_done, NB)
                pe.wait_ge(lora_done, 2 * K * DC)

                def up(g, f):
                    at = g * FC + f - 1
                    if f >= 2:
                        pe.wait_ge(h_done, at)
                    else:
                        pe.wait_ge(h_done, g * FC)
                    for k in range(K):
                        for c in range(DC):
                            m = pe.matmul(up_ps[f % 2][k][:, 0, 0:GT], W[:, k, c, f * 128:(f + 1) * 128],
                                          xnT[:, c, bass.ts(g, GT)], start=(c == 0), stop=(c == DC - 1))
                    m.then_inc(up_out, 1)

                def down(g, f):
                    pe.wait_ge(h_done, g * FC + f + 1)
                    if f == 0:
                        pe.wait_ge(dn_done, g * GB)
                    for t in range(GB):
                        m = pe.matmul(dn_ps[t][0:S, 0, 0:D], hT[:, f % RING, t * S:(t + 1) * S], wo[:, f, :],
                                      start=(f == 0), stop=(f == FC - 1))
                    m.then_inc(dn_step, 1)
                with pe.Fori(0, GROUPS) as g:
                    for f in range(FC):
                        up(g, f)
                        if f >= 1:
                            down(g, f - 1)
                    down(g, FC - 1)


def ternary_ffn(core):
    nc, ins = core.nc, core.ins
    x, ident = core.x, core.ident
    MAGIC = 1.5 * 2.0 ** 23
    SP = S + 2
    with ExitStack() as ctx:
        def sb(name, shape, dt=F32):
            return core.sb(ctx, "tf_" + name, shape, dt)

        def sem(name):
            return core.sem(ctx, "tf_" + name)

        w1, w2 = sb("w1", [128, DC * FF]), sb("w2", [128, FC * D])
        q1, q2 = sb("q1", [128, DC, FF], BF16), sb("q2", [128, FC, D], BF16)
        cw, cws, cb = sb("cw", [128, FC, 3]), sb("cws", [128, FC, 3]), sb("cb", [128, FC])
        ones, identb = sb("ones", [128, 128]), sb("identb", [128, 128], BF16)
        wsum, wmean, wscale = sb("wsum", [128, 2]), sb("wmean", [128, 2]), sb("wscale", [128, 2])
        xn, xq = sb("xn", [S, 2, D]), sb("xq", [S, 2, D], BF16)
        amax, scale = sb("amax", [S, 2, 1]), sb("scale", [S, 2, 1])
        invw = sb("invw", [S, 2, 128])
        xqT = sb("xqT", [128, DC, NB * S], BF16)
        invb = sb("invb", [128, NB * S])
        hb = sb("hb", [128, 2, GB, SP])
        t1, t2, t3 = (sb(n, [128, 2, GB, S]) for n in ("t1", "t2", "t3"))
        act_sb = sb("act", [128, FC, GT])
        am = sb("am", [128, GT])
        hmax, hscale = sb("hmax", [S, GB]), sb("hscale", [S, GB])
        hinv = sb("hinv", [S, GB])
        wide_scale = sb("wide_scale", [S, GB, 128])
        scb = sb("scb", [128, GT])
        hq = sb("hq", [128, FC, GT], BF16)
        tq_ps = [ctx.enter_context(nc.psum_tensor(f"tf_tq{i}", [128, 1, 1024], BF16)) for i in range(2)]
        inv_ps = [core.banks(ctx, f"tf_inv{i}", 1) for i in range(2)]
        up_ps = [core.banks(ctx, f"tf_up{i}", 1) for i in range(2)]
        dn_ps = core.banks(ctx, "tf_dn", 2)
        w_in, std_done, setup, wsum_out, wq_done = (sem(n) for n in ("w_in", "std", "setup", "wsum_out", "wq"))
        xq_done, xq_out, xq_taken = sem("xq"), sem("xq_out"), sem("xq_taken")
        up_out, hb_done, t1_done, t3_done, act_done = (sem(n) for n in ("up_out", "hb", "t1", "t3", "act"))
        am_done, am_out, hs_done, hs_out, hq_done, dn_out, dn_done = (
            sem(n) for n in ("am", "am_out", "hs", "hs_out", "hq", "dn_out", "dn"))
        chain = sem("chain")

        with nc.Block() as block:
            @block.sync
            def _(sp):
                for to, src in ((w1[:, :], ins["L3_ffn_w1"]), (w2[:, :], ins["L3_ffn_w2"]),
                                (cw[:, :, :], ins["L3_ffn_conv_w"]), (cb[:, :], ins["L3_ffn_conv_b"])):
                    sp.dma_start(to, src).then_inc(w_in, 16)

            @block.gpsimd
            def _(pool):
                pool.memset(ones[:, :], 1.0).then_inc(setup, 1)
                pool.memset(hb[:, :, :, :], 0.0).then_inc(setup, 1)

            @block.scalar
            def _(act):
                act.activation(core.std[:, :], core.mv[:, :, 1], ACT.Sqrt, bias=core.eps[0:S, :]).then_inc(std_done, 1)
                act.wait_ge(wq_done, 3)
                with act.Fori(0, GROUPS) as g:
                    for f in range(FC):
                        act.wait_ge(hb_done, g * FC + f + 1)
                        act.activation(t1[:, f % 2, :, :], hb[:, f % 2, :, 1:S + 1], ACT.Identity,
                                       bias=cb[:, f:f + 1], scale=cws[:, f, 1:2]).then_inc(t1_done, 1)
                        if f >= 1:
                            act.wait_ge(t3_done, g * FC + f)
                            if f == 1:
                                act.wait_ge(hq_done, g)
                            act.activation(act_sb[:, f - 1, :], t3[:, (f - 1) % 2, :, :].rearrange("p b s -> p (b s)"),
                                           ACT.Silu).then_inc(act_done, 1)
                    act.wait_ge(t3_done, (g + 1) * FC)
                    act.activation(act_sb[:, FC - 1, :], t3[:, (FC - 1) % 2, :, :].rearrange("p b s -> p (b s)"),
                                   ACT.Silu).then_inc(act_done, 1)

            @block.vector
            def _(dve):
                ch = Chain(dve, chain)
                dve.tensor_copy(identb[:, :], ident[:, :])
                dve.wait_ge(std_done, 1)
                ch.link(dve.reciprocal(core.rstd[:, :], core.std[:, :]))
                dve.wait_ge(w_in, 64)
                for n, w in enumerate((w1, w2)):
                    ch.step(dve.tensor_reduce(wsum[:, n:n + 1], w[:, :], AX.X, ALU.add, apply_absolute_value=True))
                dve.wait_ge(wsum_out, 1)
                ch.link(dve.tensor_scalar(wmean[:, :], inv_ps[0][:, 0, 0:2], 1.0 / (D * FF), EPS, ALU.mult, ALU.max))
                ch.link(dve.reciprocal(wscale[:, :], wmean[:, :]))
                for n, (w, q) in enumerate(((w1, q1), (w2, q2))):
                    ch.link(dve.tensor_scalar(w[:, :], w[:, :], wscale[:, n:n + 1], 1.0, ALU.mult, ALU.min))
                    ch.link(dve.tensor_scalar(w[:, :], w[:, :], -1.0, MAGIC, ALU.max, ALU.add))
                    dve.tensor_scalar(q[:, :, :].rearrange("p a b -> p (a b)"), w[:, :], MAGIC, None,
                                      ALU.subtract).then_inc(wq_done, 1)
                dve.tensor_scalar(cws[:, :, :], cw[:, :, :], wmean[:, 0:1], None, ALU.mult).then_inc(wq_done, 1)
                dve.wait_ge(wq_done, 3)
                dve.wait_ge(setup, 2)

                start = ch.n
                PERB = 7

                def spread(b, h):
                    c = Chain(dve, chain, start + b * PERB)
                    after(dve, xq_out, b - 1)
                    c.link(dve.tensor_scalar(xn[:, h, :], x[:, b, :], core.mv[:, b, 0:1], core.rstd[:, bass.ts(b, 1)],
                                             ALU.subtract, ALU.mult))
                    c.link(dve.tensor_reduce(amax[:, h, :], xn[:, h, :], AX.X, ALU.max, apply_absolute_value=True))
                    c.link(dve.tensor_scalar(amax[:, h, :], amax[:, h, :], EPS, 1.0 / 127.0, ALU.max, ALU.mult))
                    c.step(dve.tensor_scalar(invw[:, h, :], ones[0:S, :], amax[:, h, :], None, ALU.mult))
                    c.link(dve.reciprocal(scale[:, h, :], amax[:, h, :]))
                    c.link(dve.tensor_scalar(xn[:, h, :], xn[:, h, :], scale[:, h, :], 127.0, ALU.mult, ALU.min))
                    c.link(dve.tensor_scalar(xn[:, h, :], xn[:, h, :], -128.0, MAGIC, ALU.max, ALU.add))
                    dve.tensor_scalar(xq[:, h, :], xn[:, h, :], MAGIC, None, ALU.subtract).then_inc(xq_done, 1)
                    assert c.n == PERB
                    if not (isinstance(b, int) and b == 0):
                        take(b - 1, 1 - h)

                def take(b, h):
                    dve.wait_ge(xq_out, b + 1)
                    dve.tensor_scalar(xqT[:, :, bass.ts(b, S)], tq_ps[h][:, 0, 0:DC * S].rearrange(
                        "p (c s) -> p c s", c=DC), 1.0, None, ALU.mult)
                    dve.tensor_scalar(invb[:, bass.ts(b, S)], inv_ps[h][:, 0, 0:S], 1.0, None, ALU.mult).then_inc(xq_taken, 1)
                each_batch(dve, spread)
                take(NB - 1, 1)
                dve.wait_ge(xq_taken, NB)

                start2 = start + NB * PERB
                PER = FC + 4 + 3 + GB * core.KEEPS
                with dve.Fori(0, GROUPS) as g:
                    c = Chain(dve, chain, start2 + g * PER)

                    def take_up(f):
                        dve.wait_ge(t3_done, g * FC + max(f - 1, 0))
                        dve.wait_ge(up_out, g * FC + f + 1)
                        dve.tensor_tensor(hb[:, f % 2, :, 1:S + 1],
                                          up_ps[f % 2][:, 0, 0:GT].rearrange("p (b s) -> p b s", b=GB),
                                          invb[:, bass.ts(g, GT)].rearrange("p (b s) -> p b s", b=GB),
                                          ALU.mult).then_inc(hb_done, 1)

                    def convolve(f):
                        dve.wait_ge(t1_done, g * FC + f + 1)
                        c.link(dve.scalar_tensor_tensor(out=t2[:, f % 2, :, :], in0=hb[:, f % 2, :, 0:S],
                                                        scalar=cws[:, f, 0:1], in1=t1[:, f % 2, :, :],
                                                        op0=ALU.mult, op1=ALU.add))
                        after(dve, act_done, g * FC + f - 1) if f >= 1 else dve.wait_ge(act_done, g * FC)
                        dve.scalar_tensor_tensor(out=t3[:, f % 2, :, :], in0=hb[:, f % 2, :, 2:SP],
                                                 scalar=cws[:, f, 2:3], in1=t2[:, f % 2, :, :],
                                                 op0=ALU.mult, op1=ALU.add).then_inc(t3_done, 1)
                    for f in range(FC):
                        take_up(f)
                        if f >= 1:
                            convolve(f - 1)
                    convolve(FC - 1)
                    dve.wait_ge(act_done, (g + 1) * FC)
                    dve.tensor_reduce(am[:, :], act_sb[:, :, :].rearrange("p f t -> p t f"), AX.X, ALU.max,
                                      apply_absolute_value=True).then_inc(am_done, 1)
                    dve.wait_ge(am_out, g + 1)
                    c.link(dve.tensor_reduce(hmax[:, :], inv_ps[1][0:S, 0, :].rearrange("p (t q) -> p t q", t=GB), AX.X, ALU.max))
                    c.link(dve.tensor_scalar(hmax[:, :], hmax[:, :], EPS, 1.0 / 127.0, ALU.max, ALU.mult))
                    c.link(dve.reciprocal(hscale[:, :], hmax[:, :]))
                    c.step(dve.tensor_scalar(hinv[:, :], hmax[:, :], wmean[0:S, 1:2], None, ALU.mult))
                    dve.tensor_copy(wide_scale[:, :, :], hscale[:, :].unsqueeze(2).broadcast_to([S, GB, 128])).then_inc(hs_done, 1)
                    dve.wait_ge(hs_out, g + 1)
                    c.link(dve.tensor_copy(scb[:, :], inv_ps[0][:, 0, 0:GT]))
                    c.link(dve.tensor_tensor(act_sb[:, :, :], act_sb[:, :, :],
                                             scb[:, :].unsqueeze(1).broadcast_to([128, FC, GT]), ALU.mult))
                    c.link(dve.tensor_scalar(act_sb[:, :, :], act_sb[:, :, :], 127.0, -128.0, ALU.min, ALU.max))
                    dve.tensor_scalar(hq[:, :, :], act_sb[:, :, :], MAGIC, MAGIC, ALU.add, ALU.subtract).then_inc(hq_done, 1)
                    for t in range(GB):
                        dve.wait_ge(dn_out, g * GB + t + 1)
                        b = GB * g + t
                        dve.scalar_tensor_tensor(out=core.xs[:, t % 2, :], in0=dn_ps[0:S, t % 2, 0:D],
                                                 scalar=hinv[:, t:t + 1], in1=x[:, b, :], op0=ALU.mult,
                                                 op1=ALU.add).then_inc(dn_done, 1)
                        dve.wait_ge(dn_done, g * GB + t + 1)
                        core.keep(c, dve, b, t % 2)
                    assert c.n == PER, (c.n, PER)

            @block.tensor
            def _(pe):
                pe.wait_ge(setup, 2)
                pe.wait_ge(chain, 3)
                pe.matmul(inv_ps[0][:, 0, 0:2], ones[:, :], wsum[:, :], start=True, stop=True).then_inc(wsum_out, 1)

                pe.wait_ge(wq_done, 3)

                def turn(b, h):
                    pe.wait_ge(xq_done, b + 1)
                    after(pe, xq_taken, b - 1)
                    for c in range(DC):
                        pe.transpose(tq_ps[h][:, 0, c * S:(c + 1) * S], xq[:, h, c * 128:(c + 1) * 128], identb[0:S, 0:S])
                    pe.matmul(inv_ps[h][:, 0, 0:S], invw[:, h, :], ident[0:S, 0:S], start=True, stop=True).then_inc(xq_out, 1)
                each_batch(pe, turn)
                pe.wait_ge(xq_taken, NB)
                with pe.Fori(0, GROUPS) as g:
                    for f in range(FC):
                        pe.wait_ge(hb_done, g * FC + f - 1) if f >= 2 else pe.wait_ge(hb_done, g * FC)
                        for c in range(DC):
                            m = pe.matmul(up_ps[f % 2][:, 0, 0:GT], q1[:, c, f * 128:(f + 1) * 128],
                                          xqT[:, c, bass.ts(g, GT)], start=(c == 0), stop=(c == DC - 1))
                        m.then_inc(up_out, 1)
                    pe.wait_ge(am_done, g + 1)
                    for t in range(GB):
                        m = pe.transpose(inv_ps[1][0:S, 0, t * 128:(t + 1) * 128], am[:, t * S:(t + 1) * S], ident[:, :])
                    m.then_inc(am_out, 1)
                    pe.wait_ge(hs_done, g + 1)
                    for t in range(GB):
                        m = pe.matmul(inv_ps[0][:, 0, t * S:(t + 1) * S], wide_scale[:, t, :], ident[0:S, 0:S],
                                      start=True, stop=True)
                    m.then_inc(hs_out, 1)
                    pe.wait_ge(hq_done, g + 1)
                    for t in range(GB):
                        pe.wait_ge(dn_done, g * GB + t - 1) if t >= 2 else pe.wait_ge(dn_done, g * GB)
                        for f in range(FC):
                            m = pe.matmul(dn_ps[0:S, t % 2, 0:D], hq[:, f, t * S:(t + 1) * S], q2[:, f, :],
                                          start=(f == 0), stop=(f == FC - 1))
                        m.then_inc(dn_out, 1)


class Routing:

    def __init__(self, core, ctx, pre, rows, blocks):
        self.R, self.blocks = rows, blocks
        self.TR = 112 if rows % 112 == 0 else 128
        self.xf = core.sb(ctx, pre + "_xf", [S, NB, D])
        self.p = core.sb(ctx, pre + "_p", [S, 2, NB])
        self.put = core.sb(ctx, pre + "_put", [S, 2, NB], U32)
        self.get = core.sb(ctx, pre + "_get", [S, 2, NB], U32)
        self.owner = core.sb(ctx, pre + "_owner", [1, blocks], I32)
        self.xbuf = core.nc.dram_tensor(pre + "_xbuf", (rows * blocks, D), F32).ap()
        self.ybuf = core.nc.dram_tensor(pre + "_ybuf", (rows * blocks, D), F32).ap()


def each_block(eng, n, body):
    body(0, 0)
    body(1, 1)
    turns = (n - 2) // 2
    with eng.Fori(1, turns) as i:
        body(2 * i, 0)
        body(2 * i + 1, 1)
    for b in range(2 * turns, n):
        body(b, b % 2)


def route(core, pre, r, twice):
    nc, ins = core.nc, core.ins
    x, ident = core.x, core.ident
    NE = NB * E
    with ExitStack() as ctx:
        def sb(name, shape, dt=F32):
            return core.sb(ctx, pre + "r_" + name, shape, dt)

        def sem(name):
            return core.sem(ctx, pre + "r_" + name)

        wr = sb("wr", [128, DC, E])
        before, iota_e, iota_b = sb("before", [S, S]), sb("iota_e", [S, E]), sb("iota_b", [1, r.blocks])
        more = sb("more", [S, 2, D] if twice else [S, E])
        ones = sb("ones", [S, S])
        fill_w = r.R * r.blocks * D // 128 // 4
        zeros = sb("zeros", [128, fill_w])
        xn4 = sb("xn4", [S, 4, D])
        std2, rstd2 = sb("std2", [S, NB]), sb("rstd2", [S, NB])
        xn = sb("xn", [S, 2, D])
        xt = sb("xt", [128, 2, DC, S])
        lg = sb("lg", [S, NB, E])
        best, best_i = sb("best", [S, NB, 8]), sb("best_i", [S, NB, 8], U32)
        ci = sb("ci", [S, 2, NB])
        hot = sb("hot", [S, 2, NB, E])
        picked, pos, tmp = sb("picked", [S, NB, E]), sb("pos", [S, NB, E]), sb("tmp", [S, NB, E])
        tot, tot2 = sb("tot", [S, NB + 1, E]), sb("tot2", [S, NB + 1, E])
        base, base2 = sb("base", [S, E + 1]), sb("base2", [S, E + 1])
        place = sb("place", [S, 2, NB])
        slot = sb("slot", [S, 2, NB])
        kept = sb("kept", [S, 2, NB])
        gap = sb("gap", [S, NB])
        owns = sb("owns", [1, r.blocks, E - 1])
        owner_f = sb("owner_f", [1, r.blocks])
        xt_ps = [core.banks(ctx, f"{pre}r_xt{i}", 1) for i in range(2)]
        lg_ps = [core.banks(ctx, f"{pre}r_lg{i}", 1) for i in range(2)]
        cum_ps = core.banks(ctx, pre + "r_cum", 2)
        w_in, std_done, setup, chain, filled = (sem(n) for n in ("w_in", "std", "setup", "chain", "filled"))
        xn_done, x_out, x_done, l_out, l_done = (sem(n) for n in ("xn", "x_out", "x", "l_out", "l"))
        gap_done, gap_exp, picked_done, cum_out, slots_done = (
            sem(n) for n in ("gap", "gap_exp", "picked", "cum_out", "slots"))
        put_done = core.put_done[pre][0]
        NW = 5 + (1 if twice else 0)

        with nc.Block() as block:
            @block.sync
            def _(sp):
                sp.dma_start(wr[:, :, :], ins[pre + "_router"]).then_inc(w_in, 16)
                sp.dma_start(before[:, :], ins["before"]).then_inc(w_in, 16)
                sp.dma_start(iota_e[:, :], ins["iota"][0:E].partition_broadcast(S)).then_inc(w_in, 16)
                sp.dma_start(iota_b[:, :], ins["iota"][0:r.blocks].partition_broadcast(1)).then_inc(w_in, 16)
                if twice:
                    sp.dma_start(more[:, 0, :], ins[pre + "_gamma"].partition_broadcast(S)).then_inc(w_in, 16)
                    sp.dma_start(more[:, 1, :], ins[pre + "_beta"].partition_broadcast(S)).then_inc(w_in, 16)
                else:
                    sp.dma_start(more[:, :], ins[pre + "_router_b"].partition_broadcast(S)).then_inc(w_in, 16)
                sp.wait_ge(setup, 2)
                flat = r.xbuf.rearrange("(p n) d -> p (n d)", p=128)
                for q in range(4):
                    sp.dma_start(flat[:, q * fill_w:(q + 1) * fill_w], zeros[:, :]).then_inc(filled, 16)
                sp.wait_ge(filled, 64)

            @block.gpsimd
            def _(pool):
                pool.memset(ones[:, :], 1.0).then_inc(setup, 1)
                pool.memset(zeros[:, :], 0.0).then_inc(setup, 1)
                pool.wait_ge(slots_done, 1)
                pool.wait_ge(filled, 64)
                for b in range(NB):
                    for k in range(2):
                        pool.indirect_dma_start(
                            out=r.xbuf, out_offset=bass.IndirectOffsetOnAxis(r.put[:, k, b:b + 1], 0),
                            in_=r.xf[:, b, :], in_offset=None, bounds_check=r.R * r.blocks - 1,
                            oob_is_err=False).then_inc(put_done, 16)
                pool.wait_ge(put_done, 16 * 2 * NB)

            @block.scalar
            def _(act):
                act.activation(core.std[:, :], core.mv[:, :, 1], ACT.Sqrt, bias=core.eps[0:S, :]).then_inc(std_done, 1)
                if twice:
                    act.wait_ge(std_done, 2)
                    act.activation(std2[:, :], core.mv2[:, :, 1], ACT.Sqrt, bias=core.eps[0:S, :]).then_inc(std_done, 1)

                def body(b, h):
                    act.wait_ge(x_out, b + 1)
                    after(act, l_out, b - 1)
                    act.activation(xt[:, h, :, :], xt_ps[h][:, 0, 0:DC * S].rearrange("p (c s) -> p c s", c=DC),
                                   ACT.Copy).then_inc(x_done, 1)
                each_batch(act, body)
                act.wait_ge(gap_done, 1)
                act.activation(gap[:, :], gap[:, :], ACT.Exp).then_inc(gap_exp, 1)

            @block.vector
            def _(dve):
                ch = Chain(dve, chain)
                dve.wait_ge(std_done, 1)
                ch.link(dve.reciprocal(core.rstd[:, :], core.std[:, :]))
                if twice:
                    second_statistics(core, dve, ch, xn4, std_done)
                    dve.wait_ge(std_done, 3)
                    ch.link(dve.reciprocal(rstd2[:, :], std2[:, :]))
                dve.wait_ge(w_in, NW * 16)
                start = ch.n
                PER = 3 if twice else 0

                def take_logits(b, h):
                    dve.wait_ge(l_out, b + 1)
                    dve.tensor_scalar(lg[:, b, :], lg_ps[h][0:S, 0, 0:E], 1.0, None, ALU.mult).then_inc(l_done, 1)

                def body(b, h):
                    c = Chain(dve, chain, start + b * PER)
                    after(dve, x_out, b - 1)
                    if twice:
                        c.link(dve.tensor_scalar(xn4[:, h, :], x[:, b, :], core.mv[:, b, 0:1],
                                                 core.rstd[:, bass.ts(b, 1)], ALU.subtract, ALU.mult))
                        c.link(dve.tensor_scalar(xn4[:, 2 + h, :], xn4[:, h, :], core.mv2[:, b, 0:1],
                                                 rstd2[:, bass.ts(b, 1)], ALU.subtract, ALU.mult))
                        c.link(dve.tensor_tensor(xn4[:, h, :], xn4[:, 2 + h, :], more[:, 0, :], ALU.mult))
                        dve.tensor_tensor(xn[:, h, :], xn4[:, h, :], more[:, 1, :], ALU.add).then_inc(xn_done, 1)
                    else:
                        dve.tensor_scalar(xn[:, h, :], x[:, b, :], core.mv[:, b, 0:1],
                                          core.rstd[:, bass.ts(b, 1)], ALU.subtract, ALU.mult).then_inc(xn_done, 1)
                    dve.wait_ge(xn_done, b + 1)
                    dve.tensor_scalar(r.xf[:, b, :], xn[:, h, :], 1.0, None, ALU.mult)
                    if not (isinstance(b, int) and b == 0):
                        take_logits(b - 1, 1 - h)
                each_batch(dve, body)
                take_logits(NB - 1, 1)
                dve.wait_ge(l_done, NB)
                c = Chain(dve, chain, start + NB * PER)
                if twice:
                    c.link(dve.tensor_scalar(lg[:, :, :], lg[:, :, :], 10000.0, -10000.0, ALU.min, ALU.max))
                else:
                    c.link(dve.tensor_tensor(lg[:, :, :], lg[:, :, :],
                                             more[:, :].unsqueeze(1).broadcast_to([S, NB, E]), ALU.add))
                for b in range(NB):
                    m = dve.max(best[:, b, :], lg[:, b, :])
                c.link(m)
                for b in range(NB):
                    m = dve.max_index(best_i[:, b, :], best[:, b, :], lg[:, b, :])
                c.link(m)
                dve.tensor_tensor(gap[:, :], best[:, :, 1], best[:, :, 0], ALU.subtract).then_inc(gap_done, 1)
                for k in range(2):
                    c.link(dve.tensor_copy(ci[:, k, :], best_i[:, :, k]))
                    c.link(dve.tensor_tensor(hot[:, k, :, :], iota_e[:, :].unsqueeze(1).broadcast_to([S, NB, E]),
                                             ci[:, k, :].unsqueeze(2).broadcast_to([S, NB, E]), ALU.is_equal))
                dve.tensor_tensor(picked[:, :, :], hot[:, 0, :, :], hot[:, 1, :, :], ALU.add).then_inc(picked_done, 1)
                dve.wait_ge(gap_exp, 1)
                c.link(dve.tensor_scalar(r.p[:, 1, :], gap[:, :], 1.0, 1e-12 if twice else 0.0, ALU.add, ALU.add))
                c.link(dve.reciprocal(r.p[:, 0, :], r.p[:, 1, :]))
                c.link(dve.tensor_tensor(r.p[:, 1, :], gap[:, :], r.p[:, 0, :], ALU.mult))
                dve.wait_ge(cum_out, 1)
                c.link(dve.tensor_copy(tot[:, 1:NB + 1, :], cum_ps[0:S, 1, 0:NE].rearrange("p (b e) -> p b e", e=E)))
                c.link(dve.memset(tot[:, 0:1, :], 0.0))
                a, b_ = tot, tot2
                step = 1
                while step <= NB:
                    c.step(dve.tensor_copy(b_[:, 0:step, :], a[:, 0:step, :]))
                    c.link(dve.tensor_tensor(b_[:, step:NB + 1, :], a[:, step:NB + 1, :], a[:, 0:NB + 1 - step, :], ALU.add))
                    a, b_ = b_, a
                    step *= 2
                c.link(dve.tensor_tensor(pos[:, :, :], cum_ps[0:S, 0, 0:NE].rearrange("p (b e) -> p b e", e=E),
                                         a[:, 0:NB, :], ALU.add))
                if twice:
                    c.link(dve.tensor_scalar(base[:, 0:E], iota_e[:, :], float(r.R), None, ALU.mult))
                    base_of = base
                else:
                    c.link(dve.tensor_scalar(base[:, 1:E + 1], a[:, NB, :], float(r.R - 1), 1.0 / r.R, ALU.add, ALU.mult))
                    c.link(dve.tensor_scalar(base[:, 1:E + 1], base[:, 1:E + 1], 0.5 - 0.5 / r.R, 1.5 * 2.0 ** 23,
                                             ALU.subtract, ALU.add))
                    c.link(dve.tensor_scalar(base[:, 1:E + 1], base[:, 1:E + 1], 1.5 * 2.0 ** 23, None, ALU.subtract))
                    c.link(dve.memset(base[:, 0:1], 0.0))
                    p_, q_ = base, base2
                    step = 1
                    while step <= E:
                        c.step(dve.tensor_copy(q_[:, 0:step], p_[:, 0:step]))
                        c.link(dve.tensor_tensor(q_[:, step:E + 1], p_[:, step:E + 1], p_[:, 0:E + 1 - step], ALU.add))
                        p_, q_ = q_, p_
                        step *= 2
                    c.link(dve.tensor_tensor(owns[:, :, :], p_[0:1, 1:E].unsqueeze(1).broadcast_to([1, r.blocks, E - 1]),
                                             iota_b[:, :].unsqueeze(2).broadcast_to([1, r.blocks, E - 1]), ALU.is_le))
                    c.link(dve.tensor_reduce(owner_f[:, :], owns[:, :, :], AX.X, ALU.add))
                    c.step(dve.tensor_copy(r.owner[:, :], owner_f[:, :]))
                    c.link(dve.tensor_scalar(q_[:, 0:E], p_[:, 0:E], float(r.R), None, ALU.mult))
                    base_of = q_
                for k in range(2):
                    c.link(dve.tensor_tensor(tmp[:, :, :], hot[:, k, :, :], pos[:, :, :], ALU.mult))
                    c.link(dve.tensor_reduce(place[:, k, :], tmp[:, :, :], AX.X, ALU.add))
                    c.link(dve.tensor_tensor(tmp[:, :, :], hot[:, k, :, :],
                                             base_of[:, 0:E].unsqueeze(1).broadcast_to([S, NB, E]), ALU.mult))
                    c.link(dve.tensor_reduce(slot[:, k, :], tmp[:, :, :], AX.X, ALU.add))
                c.link(dve.tensor_tensor(slot[:, :, :], slot[:, :, :], place[:, :, :], ALU.add))
                if twice:
                    end = float(r.R * r.blocks)
                    c.link(dve.tensor_scalar(kept[:, :, :], place[:, :, :], float(r.R), None, ALU.is_lt))
                    c.link(dve.tensor_tensor(r.p[:, :, :], r.p[:, :, :], kept[:, :, :], ALU.mult))
                    c.link(dve.tensor_scalar(slot[:, :, :], slot[:, :, :], end, None, ALU.subtract))
                    c.link(dve.tensor_tensor(slot[:, :, :], slot[:, :, :], kept[:, :, :], ALU.mult))
                    c.link(dve.tensor_scalar(slot[:, :, :], slot[:, :, :], end, None, ALU.add))
                    c.link(dve.tensor_scalar(place[:, :, :], slot[:, :, :], end - 1, None, ALU.min))
                    c.link(dve.tensor_copy(r.get[:, :, :], place[:, :, :]))
                else:
                    c.link(dve.tensor_copy(r.get[:, :, :], slot[:, :, :]))
                dve.tensor_copy(r.put[:, :, :], slot[:, :, :]).then_inc(slots_done, 1)
                dve.wait_ge(slots_done, 1)

            @block.tensor
            def _(pe):
                pe.wait_ge(w_in, NW * 16)
                pe.wait_ge(setup, 2)

                def logits(b, h):
                    pe.wait_ge(x_done, b + 1)
                    after(pe, l_done, b - 1)
                    for c in range(DC):
                        m = pe.matmul(lg_ps[h][0:S, 0, 0:E], xt[:, h, c, :], wr[:, c, :], start=(c == 0), stop=(c == DC - 1))
                    m.then_inc(l_out, 1)

                def body(b, h):
                    pe.wait_ge(xn_done, b + 1)
                    after(pe, x_done, b - 1)
                    for c in range(DC):
                        m = pe.transpose(xt_ps[h][:, 0, c * S:(c + 1) * S], xn[:, h, c * 128:(c + 1) * 128], ident[0:S, 0:S])
                    m.then_inc(x_out, 1)
                    if not (isinstance(b, int) and b == 0):
                        logits(b - 1, 1 - h)
                each_batch(pe, body)
                logits(NB - 1, 1)
                pe.wait_ge(picked_done, 1)
                flat = picked[:, :, :].rearrange("p b e -> p (b e)")
                pe.matmul(cum_ps[0:S, 0, 0:NE], before[:, :], flat, start=True, stop=True)
                pe.matmul(cum_ps[0:S, 1, 0:NE], ones[:, :], flat, start=True, stop=True).then_inc(cum_out, 1)


def run_experts(core, pre, r, gated):
    nc, ins = core.nc, core.ins
    ident = core.ident
    R, TR, N = r.R, r.TR, r.blocks
    NT = R // TR
    HALVES = -(-R // 512)
    RH = R // HALVES
    UP = 2 * FF if gated else FF
    KINDS = 2 if gated else 1
    RING = 2 if gated else 4
    with ExitStack() as ctx:
        def sb(name, shape, dt=F32):
            return core.sb(ctx, pre + "e_" + name, shape, dt)

        def sem(name):
            return core.sem(ctx, pre + "e_" + name)

        wu, wd = sb("wu", [128, 2, DC, UP]), sb("wd", [128, 2, FC, D])
        if not gated:
            b1, b2 = sb("b1", [128, 2, FC]), sb("b2", [TR, 2, D])
        rows = sb("rows", [TR, 2, NT, D])
        xT = sb("xT", [128, 2, DC, R])
        hT = sb("hT", [128, 2, FC, R])
        if gated:
            sg = sb("sg", [128, 2, RH])
        y = sb("y", [TR, 2, D])
        up_ps = [[core.banks(ctx, f"{pre}e_up{i}{k}", 1) for k in range(KINDS)] for i in range(RING)]
        t_ps = [core.banks(ctx, f"{pre}e_t{i}", 1) for i in range(2)]
        dn_ps = [core.banks(ctx, f"{pre}e_dn{i}", 1) for i in range(2)]
        up_in, dn_in, rows_in = ([sem(f"{n}{i}") for i in range(2)] for n in ("up_in", "dn_in", "rows_in"))
        t_out, t_done, up_out, sg_done, h_done, dn_out, y_done = (
            sem(n) for n in ("t_out", "t", "up_out", "sg", "h", "dn_out", "y"))
        stored = core.stored[pre]
        UPB = FC * HALVES
        NDN = 1 if gated else 3

        def first(b):
            return isinstance(b, int) and b == 0

        def last(b):
            return isinstance(b, int) and b == N - 1

        with nc.Block() as block:
            @block.sync
            def _(sp):
                def body(b, h):
                    e = b if gated else sp.value_load(r.owner[0:1, bass.ts(b, 1)], min_val=0, max_val=E - 1)
                    after(sp, t_out, (b - 1) * NT)
                    sp.dma_start(rows[:, h, :, :], r.xbuf[bass.ts(b, R), :].rearrange("(t p) d -> p t d", p=TR)
                                 ).then_inc(rows_in[h], 16)
                    after(sp, up_out, (b - 1) * UPB)
                    sp.dma_start(wu[:, h, :, :], ins[pre + "_up"][e]).then_inc(up_in[h], 16)
                    after(sp, dn_out, (b - 1) * NT)
                    sp.dma_start(wd[:, h, :, :], ins[pre + "_down"][e]).then_inc(dn_in[h], 16)
                    if not gated:
                        after(sp, h_done, (b - 1) * UPB)
                        after(sp, y_done, (b - 1) * NT)
                        sp.dma_start(b1[:, h, :], ins[pre + "_b1"][e]).then_inc(dn_in[h], 16)
                        sp.dma_start(b2[:, h, :], ins[pre + "_b2"][e].partition_broadcast(TR)).then_inc(dn_in[h], 16)
                each_block(sp, N, body)

            @block.gpsimd
            def _(pool):
                def body(b, h):
                    for t in range(NT):
                        n = b * NT + t
                        pool.wait_ge(y_done, n + 1)
                        pool.dma_start(r.ybuf[bass.ts(n, TR), :], y[:, (h * NT + t) % 2, :]
                                       ).then_inc(stored[(h * NT + t) % 2], 16)
                each_block(pool, N, body)
                tiles = N * NT
                pool.wait_ge(stored[0], 16 * ((tiles + 1) // 2))
                pool.wait_ge(stored[1], 16 * (tiles // 2))

            def at_up(b, s):
                return b * UPB + s

            @block.scalar
            def _(act):
                def body(b, h):
                    if not gated:
                        act.wait_ge(dn_in[h], (b - h) * 24 + 48)
                    after(act, dn_out, (b - 1) * NT)
                    for s in range(UPB):
                        f, q = s // HALVES, s % HALVES
                        act.wait_ge(up_out, at_up(b, s) + 1)
                        src = up_ps[s % RING][0][:, 0, 0:RH]
                        if gated:
                            after(act, h_done, at_up(b, s) - 1)
                            act.activation(sg[:, s % 2, :], src, ACT.Silu).then_inc(sg_done, 1)
                        else:
                            act.activation(hT[:, h, f, q * RH:(q + 1) * RH], src, ACT.Gelu,
                                           bias=b1[:, h, f:f + 1]).then_inc(h_done, 1)
                each_block(act, N, body)

            @block.vector
            def _(dve):
                def take_rows(b, h):
                    for t in range(NT):
                        n = b * NT + t
                        dve.wait_ge(t_out, n + 1)
                        if t == 0:
                            after(dve, up_out, (b - 1) * UPB)
                        dve.tensor_copy(xT[:, h, :, t * TR:(t + 1) * TR],
                                        t_ps[(h * NT + t) % 2][:, 0, 0:DC * TR].rearrange("p (c s) -> p c s", c=DC)
                                        ).then_inc(t_done, 1)

                def take_results(b, h):
                    for t in range(NT):
                        n = b * NT + t
                        i = (h * NT + t) % 2
                        dve.wait_ge(dn_out, n + 1)
                        after(dve, stored[i], 16 * done_before(b, h, t))
                        if gated:
                            dve.tensor_copy(y[:, i, :], dn_ps[i][0:TR, 0, 0:D]).then_inc(y_done, 1)
                        else:
                            dve.tensor_tensor(y[:, i, :], dn_ps[i][0:TR, 0, 0:D], b2[:, h, :], ALU.add).then_inc(y_done, 1)

                def done_before(b, h, t):
                    own = sum(1 for u in range(h * NT + t) if u % 2 == (h * NT + t) % 2)
                    return (b - h) // 2 * NT + own

                def body(b, h):
                    if first(b):
                        take_rows(0, 0)
                    if not gated:
                        dve.wait_ge(dn_in[h], (b - h) * 24 + 48)
                    for s in range(UPB):
                        f, q = s // HALVES, s % HALVES
                        if gated:
                            dve.wait_ge(sg_done, at_up(b, s) + 1)
                            dve.tensor_tensor(hT[:, h, f, q * RH:(q + 1) * RH], sg[:, s % 2, :],
                                              up_ps[s % RING][1][:, 0, 0:RH], ALU.mult).then_inc(h_done, 1)
                        if s == 1 and not first(b):
                            take_results(b - 1, 1 - h)
                    if not last(b):
                        take_rows(b + 1, 1 - h)

                each_block(dve, N, body)
                take_results(N - 1, (N - 1) % 2)

            @block.tensor
            def _(pe):
                def turn_rows(b, h):
                    pe.wait_ge(rows_in[h], (b - h) * 8 + 16)
                    for t in range(NT):
                        n = b * NT + t
                        after(pe, t_done, n - 1)
                        for c in range(DC):
                            m = pe.transpose(t_ps[(h * NT + t) % 2][:, 0, c * TR:(c + 1) * TR],
                                             rows[:, h, t, c * 128:(c + 1) * 128], ident[0:TR, 0:TR])
                        m.then_inc(t_out, 1)

                def second(b, h):
                    pe.wait_ge(dn_in[h], (b - h) * 8 * NDN + 16 * NDN)
                    pe.wait_ge(h_done, (b + 1) * UPB)
                    for t in range(NT):
                        n = b * NT + t
                        i = (h * NT + t) % 2
                        after(pe, y_done, n - 1)
                        for f in range(FC):
                            m = pe.matmul(dn_ps[i][0:TR, 0, 0:D], hT[:, h, f, t * TR:(t + 1) * TR], wd[:, h, f, :],
                                          start=(f == 0), stop=(f == FC - 1))
                        m.then_inc(dn_out, 1)

                def body(b, h):
                    if first(b):
                        turn_rows(0, 0)
                    pe.wait_ge(up_in[h], (b - h) * 8 + 16)
                    pe.wait_ge(t_done, (b + 1) * NT)
                    for s in range(UPB):
                        f, q = s // HALVES, s % HALVES
                        after(pe, h_done, at_up(b, s) - RING + 1)
                        for k in range(KINDS):
                            for c in range(DC):
                                m = pe.matmul(up_ps[s % RING][k][:, 0, 0:RH],
                                              wu[:, h, c, k * FF + f * 128:k * FF + (f + 1) * 128],
                                              xT[:, h, c, q * RH:(q + 1) * RH], start=(c == 0), stop=(c == DC - 1))
                        m.then_inc(up_out, 1)
                        if s == 1 and not first(b):
                            second(b - 1, 1 - h)
                    if not last(b):
                        turn_rows(b + 1, 1 - h)
                each_block(pe, N, body)
                second(N - 1, (N - 1) % 2)


def combine(core, pre, r, norm):
    nc, ins = core.nc, core.ins
    x = core.x
    RING = 4
    with ExitStack() as ctx:
        def sb(name, shape, dt=F32):
            return core.sb(ctx, pre + "c_" + name, shape, dt)

        def sem(name):
            return core.sem(ctx, pre + "c_" + name)

        got = sb("got", [S, RING, 2, D])
        half = sb("half", [S, 2, D])
        chain, w_in, var_done, std_done, tiny_done = (sem(n) for n in ("chain", "w_in", "var", "std", "tiny"))
        got_in = core.got_in[pre]
        summed = sem("summed")
        if norm:
            wb = sb("wb", [S, 2, D])
            tiny = sb("tiny", [S, 1])
            std3, rstd3 = sb("std3", [S, NB]), sb("rstd3", [S, NB])

        with nc.Block() as block:
            if norm:
                @block.sync
                def _(sp):
                    sp.dma_start(wb[:, 0, :], ins[pre + "_ln_w"].partition_broadcast(S)).then_inc(w_in, 16)
                    sp.dma_start(wb[:, 1, :], ins[pre + "_ln_b"].partition_broadcast(S)).then_inc(w_in, 16)

            @block.gpsimd
            def _(pool):
                for b in range(NB):
                    after(pool, summed, b - RING + 1)
                    for k in range(2):
                        pool.indirect_dma_start(
                            out=got[:, b % RING, k, :], out_offset=None, in_=r.ybuf,
                            in_offset=bass.IndirectOffsetOnAxis(r.get[:, k, b:b + 1], 0)).then_inc(got_in[b % RING], 16)

            if norm:
                @block.scalar
                def _(act):
                    act.wait_ge(tiny_done, 1)
                    act.wait_ge(var_done, 1)
                    act.activation(std3[:, :], core.mv2[:, :, 1], ACT.Sqrt, bias=tiny[:, :]).then_inc(std_done, 1)

            @block.vector
            def _(dve):
                c = Chain(dve, chain)
                if norm:
                    dve.memset(tiny[:, :], 1e-12).then_inc(tiny_done, 1)
                for b in range(NB):
                    h = b % 2
                    dve.wait_ge(got_in[b % RING], 32 * (b // RING + 1))
                    to = r.xf[:, b, :] if norm else x[:, b, :]
                    c.link(dve.scalar_tensor_tensor(out=half[:, h, :], in0=got[:, b % RING, 0, :], scalar=r.p[:, 0, b:b + 1],
                                                    in1=to, op0=ALU.mult, op1=ALU.add))
                    dve.scalar_tensor_tensor(out=to, in0=got[:, b % RING, 1, :], scalar=r.p[:, 1, b:b + 1],
                                             in1=half[:, h, :], op0=ALU.mult, op1=ALU.add).then_inc(summed, 1)
                    dve.wait_ge(summed, b + 1)
                    c.link(dve.bn_stats(core.st6[:, h, :], to))
                    c.step(dve.bn_aggr((core.mv2 if norm else core.mv)[:, b, :], core.st6[:, h, :]))
                if norm:
                    dve.wait_ge(c.sem, c.n)
                    dve.sem_inc(var_done, 1)
                    dve.wait_ge(w_in, 32)
                    dve.wait_ge(std_done, 1)
                    c.link(dve.reciprocal(rstd3[:, :], std3[:, :]))
                    for b in range(NB):
                        to = r.xf[:, b, :]
                        c.link(dve.tensor_scalar(half[:, b % 2, :], to, core.mv2[:, b, 0:1], rstd3[:, b:b + 1],
                                                 ALU.subtract, ALU.mult))
                        c.link(dve.tensor_tensor(to, half[:, b % 2, :], wb[:, 0, :], ALU.mult))
                        c.link(dve.tensor_tensor(half[:, b % 2, :], to, wb[:, 1, :], ALU.add))
                        c.link(dve.tensor_tensor(x[:, b, :], half[:, b % 2, :], x[:, b, :], ALU.add))
                        c.link(dve.bn_stats(core.st6[:, b % 2, :], x[:, b, :]))
                        c.step(dve.bn_aggr(core.mv[:, b, :], core.st6[:, b % 2, :]))


def routed_experts(core, pre, gated):
    with ExitStack() as ctx:
        if gated:
            rows, blocks = -(-NB * S * 2 * 5 // (4 * E)), E
        else:
            rows = 256
            blocks = (NB * S * 2 - E) // rows + E
        r = Routing(core, ctx, pre, rows, blocks)
        route(core, pre, r, gated)
        core.clear()
        run_experts(core, pre, r, gated)
        core.clear()
        combine(core, pre, r, not gated)


def program(nc, ins, out):
    with ExitStack() as ctx:
        core = Core(nc, ctx, ins)
        load_inputs(core)
        core.clear()
        for layer in LAYERS:
            PARTS[layer](core)
            core.clear()
        store_output(core, out)


PARTS = {
    0: focused_attention,
    2: tanh_attention,
    1: lambda core: routed_experts(core, "L0_ffn", True),
    5: lambda core: routed_experts(core, "L2_ffn", False),
    3: shared_experts,
    7: ternary_ffn,
    4: lambda core: softmax_attention(core, "L2_xattn", True),
    6: lambda core: softmax_attention(core, "L3_xattn", False),
}


def kernel(**inputs):
    import concourse.bacc as _bacc
    from concourse.bass_utils import run_bass_kernel_spmd as _run

    a = {k: np.asarray(v) for k, v in inputs.items()}

    def rows_t(w, chunks):
        return w.T.reshape(chunks, 128, -1).transpose(1, 0, 2)

    def rows(w, chunks):
        return w.reshape(chunks, 128, -1).transpose(1, 0, 2)

    def stack_t(w, chunks):
        return w.transpose(0, 2, 1).reshape(E, chunks, 128, -1).transpose(0, 2, 1, 3)

    ctx = a["ctx_1024"]
    laid = {
        "x": a["x"],
        "ctxT": ctx.transpose(0, 2, 1).reshape(NB, DC, 128, SK).transpose(0, 2, 1, 3),
        "ctx_rows": ctx.reshape(NB, KT, KP, D).transpose(0, 2, 1, 3),
        "ident": np.eye(128, dtype=np.float32),
        "headmask": np.repeat(np.eye(HG, dtype=np.float32), DH, axis=0),
        "key_mask": a["mask_Bx1xS2_bk0"].reshape(NB, KT, KP).transpose(2, 0, 1),
        "L1_xattn_scale": a["L1_xattn_scale"].reshape(1),
        "L1_xattn_log_C": a["L1_xattn_log_C"].reshape(1),
        "L0_xattn_Wq": rows_t(a["L0_xattn_Wq"], DC),
        "L0_xattn_Wk": rows_t(a["L0_xattn_Wk"], DC),
        "L0_xattn_Wv": rows_t(a["L0_xattn_Wv"], DC),
        "L0_xattn_Wp": rows_t(a["L0_xattn_Wp"], DC),
        "L0_xattn_focus": a["L0_xattn_focusing_factor"].reshape(1),
        "tag": (0x80000000 + DH - 1 - np.arange(D) % DH).astype(np.uint32),
        "kvmask": np.concatenate([np.kron(np.eye(HG), np.ones((DH, DH))) / S,
                                  np.repeat(np.eye(HG), DH, axis=0) / SK], axis=1).astype(np.float32),
        "before": np.triu(np.ones((S, S), np.float32), 1),
        "iota": np.arange(32, dtype=np.float32),
        "L0_ffn_router": rows_t(a["L0_ffn_router_w"], DC),
        "L0_ffn_gamma": a["L0_ffn_ln_gamma"],
        "L0_ffn_beta": a["L0_ffn_ln_beta"],
        "L0_ffn_up": stack_t(a["L0_ffn_w12"], DC),
        "L0_ffn_down": stack_t(a["L0_ffn_w3"], FC),
        "L2_ffn_router": rows_t(a["L2_ffn_router_w"], DC),
        "L2_ffn_router_b": a["L2_ffn_router_b"],
        "L2_ffn_up": stack_t(a["L2_ffn_w1"], DC),
        "L2_ffn_down": stack_t(a["L2_ffn_w2"], FC),
        "L2_ffn_b1": a["L2_ffn_b1"].reshape(E, FC, 128).transpose(0, 2, 1),
        "L2_ffn_b2": a["L2_ffn_b2"],
        "L2_ffn_ln_w": a["L2_ffn_ln_w"],
        "L2_ffn_ln_b": a["L2_ffn_ln_b"],
        "L1_ffn_A": a["L1_ffn_lora_As"].reshape(128, D),
        "L1_ffn_B": a["L1_ffn_lora_Bs"].transpose(0, 2, 1).reshape(128, FF),
        "rank_expert": np.repeat(np.arange(E), 128 // E).astype(np.float32).reshape(128, 1),
        "L1_ffn_chosen": a["L1_ffn_top_k_indices"],
        "L1_ffn_values": a["L1_ffn_top_k_values"],
        "L1_ffn_wi": rows_t(a["L1_ffn_wi_w"], DC),
        "L1_ffn_wo": rows_t(a["L1_ffn_wo_w"], FC),
        "L3_ffn_w1": rows_t(a["L3_ffn_w1"], DC).reshape(128, DC * FF),
        "L3_ffn_w2": rows_t(a["L3_ffn_w2"], FC).reshape(128, FC * D),
        "L3_ffn_conv_w": a["L3_ffn_conv_w"].reshape(FC, 128, 3).transpose(1, 0, 2),
        "L3_ffn_conv_b": a["L3_ffn_conv_b"].reshape(FC, 128).T,
        "L1_xattn_W_outT": rows_t(a["L1_xattn_W_out"], DC),
        "L2_xattn_Wq": rows(a["L2_xattn_w_q"], DC),
        "L2_xattn_Wk": rows(a["L2_xattn_w_kv"][:, :1024], DC),
        "L2_xattn_Wv": rows(a["L2_xattn_w_kv"][:, 1024:], DC),
        "L2_xattn_Wo": rows(a["L2_xattn_w_out"], 8),
        "L2_xattn_bo": a["L2_xattn_b_out"],
        "L2_xattn_gamma": a["L2_xattn_ln_gamma"].reshape(DC, 128).T,
        "L2_xattn_beta": a["L2_xattn_ln_beta"].reshape(DC, 128).T,
        "L2_xattn_gate": a["L2_xattn_gate"],
        "L3_xattn_Wq": rows_t(a["L3_xattn_Wq"], DC),
        "L3_xattn_Wk": rows_t(a["L3_xattn_Wk"], DC),
        "L3_xattn_Wv": rows_t(a["L3_xattn_Wv"], DC),
        "L3_xattn_Wo": rows_t(a["L3_xattn_Wo"], DC),
        "L3_xattn_bq": a["L3_xattn_bq"].reshape(DC, 128).T,
        "L3_xattn_bk": a["L3_xattn_bk"].reshape(DC, 128).T,
        "L3_xattn_bv": a["L3_xattn_bv"],
        "L3_xattn_bo": a["L3_xattn_bo"],
        "mask": a["mask_BxSxS2_if1"],
    }
    nc = _bacc.Bacc("TRN2", target_bir_lowering=False, num_devices=1)
    arrays, ins = {}, {}
    for name, v in laid.items():
        v = np.ascontiguousarray(v)
        arrays[f"in_{name}"] = v
        ins[name] = nc.dram_tensor(f"in_{name}", v.shape, mybir.dt.from_np(v.dtype), kind="ExternalInput").ap()
    out = nc.dram_tensor("out_0", (NB, S, D), F32, kind="ExternalOutput").ap()
    program(nc, ins, out)
    r = _run(nc, [arrays], core_ids=[0])
    return r.results[0]["out_0"]
```
